# Optimizing a Trainium2 kernel written in Bass

```python
import numpy as np
import jax
import jax.numpy as jnp

def _softmax(x, axis=-1):
    return jax.nn.softmax(x, axis=axis)
def _gelu(x):
    return jax.nn.gelu(x, approximate=True)
def _silu(x):
    return jax.nn.silu(x)
def _sigmoid(x):
    return jax.nn.sigmoid(x)
def _layernorm(x, axis=-1, eps=1e-5):
    m = jnp.mean(x, axis=axis, keepdims=True)
    v = jnp.var(x, axis=axis, keepdims=True)
    return (x - m) / jnp.sqrt(v + eps)
def _scatter_add(tgt, idx, src, axis=0):
    return tgt.at[idx].add(src)
def _segment_sum(src, seg, n):
    return jax.ops.segment_sum(src, seg, n)

kernel_name = 'mk_conv_seq_d1_conv_nchw16_fcec8b'

def setup_inputs(seed: int = 0):
    np.random.seed(seed)
    _w = jnp.asarray
    def _rec_inputs():
        import jax
        import jax.numpy as jnp
        _gk = jax.random.key(seed)
        x = -0.003879 + 1.002 * jax.random.normal(jax.random.fold_in(_gk, 1), (1, 16, 88, 88), jnp.float32)
        return x
    x = _rec_inputs()
    def _L0_conv_setup():
        import jax, jax.numpy as jnp
        import numpy as np
        NMEM, NSEQ, C, WF, HF = (30, 16, 256, 22, 22)
        WL, HL = (88, 88)
        ALPHA = 20.0

        def _bilinear(x, size):
            return jax.image.resize(x, x.shape[:-2] + tuple(size), method='bilinear', antialias=False)
        key = jax.random.key(seed)
        k1, k2, k3, k4 = jax.random.split(key, 4)
        return {'test_scores': jax.random.normal(k1, (1, NSEQ, WL, HL), jnp.float32), 'train_labels': jax.random.uniform(k2, (NMEM, NSEQ, WL, HL), jnp.float32), 'test_feat': jax.random.normal(k3, (1, NSEQ, C, WF, HF), jnp.float32), 'train_feats': jax.random.normal(k4, (NMEM, NSEQ, C, WF, HF), jnp.float32), 'softmax_temp': jnp.full((1,), 50.0, jnp.float32)}
    _L0_conv_all = _L0_conv_setup()
    _L0_conv_in = {k: v for k, v in _L0_conv_all.items() if k in ('train_labels', 'test_feat', 'train_feats', 'softmax_temp', )}
    del _L0_conv_all

    return {
        "x": x,
        "L0_conv_train_labels": _L0_conv_in["train_labels"],
        "L0_conv_test_feat": _L0_conv_in["test_feat"],
        "L0_conv_train_feats": _L0_conv_in["train_feats"],
        "L0_conv_softmax_temp": _L0_conv_in["softmax_temp"],
    }

def reference(x, L0_conv_train_labels, L0_conv_test_feat, L0_conv_train_feats, L0_conv_softmax_temp):
    import jax
    import jax.numpy as jnp
    def _L0_conv_ref(test_scores, train_labels, test_feat, train_feats, softmax_temp):
        import jax, jax.numpy as jnp
        import numpy as np
        NMEM, NSEQ, C, WF, HF = (30, 16, 256, 22, 22)
        WL, HL = (88, 88)
        ALPHA = 20.0

        def _bilinear(x, size):
            return jax.image.resize(x, x.shape[:-2] + tuple(size), method='bilinear', antialias=False)
        nmem, nseq, c, wf, hf = train_feats.shape
        _, _, wl, hl = test_scores.shape
        p2 = wf * hf
        tr = jnp.transpose(train_feats, (1, 2, 0, 3, 4)).reshape(nseq, c, nmem * p2)
        te = jnp.transpose(test_feat, (1, 2, 0, 3, 4)).reshape(nseq, c, p2)
        tr = tr / jnp.sqrt(jnp.einsum('bij,bij->bj', tr, tr))[:, None, :]
        te = te / jnp.sqrt(jnp.einsum('bij,bij->bj', te, te))[:, None, :]
        sim = jnp.einsum('bij,bik->bjk', te, tr)
        sim = sim.reshape(nseq, p2, nmem, p2).transpose(2, 0, 1, 3)
        labels_down = _bilinear(train_labels, (wf, hf)).reshape(nmem, nseq, p2)
        p = jax.nn.softmax(softmax_temp * sim, axis=3)
        pmt_down = jnp.einsum('mnij,mnj->mni', p, labels_down).reshape(nmem, nseq, wf, hf)
        pmt = _bilinear(pmt_down, (wl, hl))
        mean = jnp.mean(pmt, axis=0, keepdims=True)
        std = jnp.std(pmt, axis=0, ddof=1, keepdims=True)
        certainty = jnp.exp(ALPHA / (1.0 + std ** 2) - ALPHA)
        return certainty * mean + test_scores

    def _gn(v, G=8, eps=1e-5):
        B_, C_, H_, W_ = v.shape
        g = v.reshape(B_, G, C_ // G, H_, W_)
        m = jnp.mean(g, axis=(2, 3, 4), keepdims=True)
        s = jnp.var(g, axis=(2, 3, 4), keepdims=True)
        return ((g - m) / jnp.sqrt(s + eps)).reshape(v.shape)

    def _ln_c(v, eps=1e-6):
        m = jnp.mean(v, axis=1, keepdims=True)
        s = jnp.var(v, axis=1, keepdims=True)
        return (v - m) / jnp.sqrt(s + eps)

    def _ln_t(v, eps=1e-5):
        m = jnp.mean(v, axis=-1, keepdims=True)
        s = jnp.var(v, axis=-1, keepdims=True)
        return (v - m) / jnp.sqrt(s + eps)

    def _to_tokens(v):
        B_, C_, H_, W_ = v.shape
        return v.reshape(B_, C_, H_ * W_).transpose(0, 2, 1)
    def _from_tokens(t, like):
        B_, C_, H_, W_ = like.shape
        return t.transpose(0, 2, 1).reshape(B_, C_, H_, W_)

    x = _L0_conv_ref(x, L0_conv_train_labels, L0_conv_test_feat, L0_conv_train_feats, L0_conv_softmax_temp)
    return x


_drawn_inputs = setup_inputs


def setup_inputs(seed=0):
    import zlib

    import numpy as np

    out = dict(_drawn_inputs(seed))
    spreads = {}
    factors = {'L0_conv_train_labels': 6.938, 'L0_conv_test_feat': 6.713, 'L0_conv_train_feats': 6.945}
    for name, (base, spread) in spreads.items():
        noise = np.random.default_rng([zlib.crc32(name.encode()), seed]).standard_normal(out[name].shape)
        drawn = base * np.exp(spread * noise) if base else spread * noise
        out[name] = jnp.asarray(drawn.astype(out[name].dtype))
    for name, factor in factors.items():
        out[name] = (out[name] * factor).astype(out[name].dtype)
    return out
```

```python
from contextlib import ExitStack

import concourse.bass as bass
from concourse import mybir

ALU = mybir.AluOpType
ACT = mybir.ActivationFunctionType
AX = mybir.AxisListType
F32 = mybir.dt.float32
F32R = mybir.dt.float32r
I32 = mybir.dt.int32
BF16 = mybir.dt.bfloat16

P = 128
NMEM, NSEQ, C, WF, HF = 30, 16, 256, 22, 22
WL, HL = 88, 88
PIX = WF * HF
CC = C // P
KT = 4
KP = PIX // KT
ZC = 32
U = 6
BODIES = NMEM // U
PAIRS = NMEM * NSEQ
NCOL = PAIRS + NSEQ
AHEAD = U - 1
ROWS = NMEM // 2
WIN = 5
WP = WIN * WF
WINDOWS = [4 * w for w in range(5)] + [HF - WIN]
IMG = 120
BATCHES = NMEM * NSEQ // IMG
UPS = 4
VAR = 16 + 2
ALPHA = 20.0
STEPS = 3
RSQ = 3 + 3 * STEPS
MAGIC = 0x5F3759DF


def upsampling():
    import numpy as np

    def line(n_in, n_out):
        w = np.zeros((n_in, n_out), np.float32)
        for o in range(n_out):
            at = (o + 0.5) * n_in / n_out - 0.5
            lo = int(np.floor(at))
            for i, f in ((lo, 1 - (at - lo)), (lo + 1, at - lo)):
                w[min(max(i, 0), n_in - 1), o] += f
        return w

    rows = line(WF, WL)
    up = np.zeros((WIN, WF, VAR, WL), np.float32)
    for k in range(16):
        v, f = k // UPS, (k % UPS + 0.5) / UPS
        up[v, :, k] = (1 - f) * rows
        up[v + 1, :, k] = f * rows
    up[0, :, 16] = rows
    up[WIN - 1, :, 17] = rows
    return up.reshape(WP, VAR * WL)


def selector():
    import numpy as np

    s = np.zeros((KT, ZC // 2, 2, 2, ZC // 2), np.float32)
    for r in range(ZC // 2):
        for d in range(2):
            s[:, r, d, d, r] = 1.0
    return s.reshape(P, ZC)


def build(nc, x, labels, test_feat, train_feats, temp, c_ident, c_sel, c_up, out):
    with ExitStack() as ctx:
        def sb(name, shape, dt=F32):
            return ctx.enter_context(nc.sbuf_tensor(name, shape, dt))

        def ps(name, shape):
            return ctx.enter_context(nc.psum_tensor(name, shape, F32))

        def sem(name):
            return ctx.enter_context(nc.semaphore(name))

        raw_all = sb("raw_all", [P, U, CC, PIX])
        raw = [raw_all[:, s] for s in range(U)]
        hi = [sb(f"hi{s}", [P, CC, PIX], F32R) for s in range(U)]
        lo = [sb(f"lo{s}", [P, CC, PIX], F32R) for s in range(U)]
        sq = [sb(f"sq{s}", [P, CC, PIX]) for s in range(2)]
        sumsq = [sb(f"sumsq{s}", [P, KT, P]) for s in range(2)]
        norms = sb("norms", [P, 2 * KT, 32])
        seed = sb("seed", [P, 2 * KT])
        root_a = sb("root_a", [P, 2 * KT])
        root_b = sb("root_b", [P, 2 * KT])
        rk = [sb(f"rk{s}", [P, 2 * KT]) for s in range(U // 2)]
        prob = [sb(f"prob{s}", [KP, KT, PIX]) for s in range(2)]
        lab = sb("lab", [KP, NMEM * NSEQ, KT])
        z_all = sb("z_all", [KP, ROWS * 258])
        z = [sb(f"z{s}", [KP, KT * ZC]) for s in range(2)]
        z_zero = sb("z_zero", [KP, ZC])
        te_raw = sb("te_raw", [P, CC, PIX])
        te_sq = sb("te_sq", [P, CC, PIX])
        te_ss = sb("te_ss", [P, PIX])
        te_r = sb("te_r", [P, PIX])
        te_a = sb("te_a", [P, PIX])
        te_b = sb("te_b", [P, PIX])
        te_hi = sb("te_hi", [P, CC, PIX], F32R)
        te_lo = sb("te_lo", [P, CC, PIX], F32R)
        sums = [sb(f"sums{g}", [P, PIX]) for g in range(2)]
        rden = sb("rden", [WP, 6, 2, ROWS])
        down = sb("down", [WP, 6, NSEQ * NMEM + NSEQ])
        ident = sb("ident", [P, P])
        ones = sb("ones", [P, P])
        sel = sb("sel", [P, ZC])
        tempc = sb("tempc", [P, 1])

        s_bank = [ps(f"s_bank{b}", [P, 512]) for b in range(KT)]
        n_bank = ps("n_bank", [P, 512])
        pv_bank = [ps(f"pv_bank{g}", [P, 512]) for g in range(2)]
        m_bank = ps("m_bank", [P, 512])

        const_in = sem("const_in")
        lab_in = sem("lab_in")
        te_in = sem("te_in")
        tr_in = [sem(f"tr_in{s}") for s in range(U)]
        x_in = sem("x_in")
        inited = sem("inited")
        lab_sum = sem("lab_sum")
        lab_turned = sem("lab_turned")
        lab_kept = sem("lab_kept")
        squared = sem("squared")
        rounded = sem("rounded")
        rest = sem("rest")
        added = sem("added")
        normed = sem("normed")
        root = sem("root")
        scored = sem("scored")
        exped = sem("exped")
        z_ready = sem("z_ready")
        z_built = sem("z_built")
        weighed = sem("weighed")
        kept = sem("kept")
        gathered = sem("gathered")
        divided = sem("divided")
        te_squared = sem("te_squared")
        te_added = sem("te_added")
        te_summed = sem("te_summed")
        te_root = sem("te_root")
        te_scaled = sem("te_scaled")
        te_rounded = sem("te_rounded")
        te_ready = sem("te_ready")
        centred = sem("centred")
        upped = sem("upped")
        up_squared = sem("up_squared")
        up_read = sem("up_read")
        up_reduced = sem("up_reduced")
        tail = sem("tail")
        tail_exp = sem("tail_exp")
        out_done = sem("out_done")

        tr_v = train_feats.rearrange("m n (p c) h w -> m n p c (h w)", c=CC)
        te_v = test_feat.rearrange("o n (p c) h w -> (o n) p c (h w)", c=CC)
        lab_v = labels.rearrange("m n (y r) x -> (m n) y r x", r=UPS)

        flat = raw_all[:, :, :, :].rearrange("p u c k -> p (u c k)")
        lab_raw = flat[0:IMG, 0:WF * 2 * HL].rearrange("p (y r x) -> p y r x", r=2, x=HL)
        lab_rows = sb("lab_rows", [IMG, WF, HF, 2])
        lab_down = sb("lab_down", [IMG, PIX])

        up32 = flat[0:WP, 0:VAR * WL].rearrange("p (v y) -> p v y", v=VAR)
        at = VAR * WL
        xin, mean, var = (
            flat[0:WL, at + NSEQ * HL * b:at + NSEQ * HL * (b + 1)].rearrange("p (n x) -> p n x", x=HL)
            for b in range(3)
        )
        up = sb("up", [WP, VAR, WL], F32R)
        down_hi = sb("down_hi", [WP, 6, NSEQ * NMEM + NSEQ], F32R)
        down_lo = sb("down_lo", [WP, 6, NSEQ * NMEM + NSEQ], F32R)
        up_sq = [prob[b][0:WL, 0, 0:NSEQ * NMEM] for b in range(2)]

        xm = sb("xm", [WL, NSEQ * HL])
        zeros = sb("zeros", [P, 512], BF16)
        bias = sb("bias", [P, 1])
        z_rows = z_all[:, :].rearrange("p (r x) -> p r x", r=ROWS)
        z_labels = z_rows[:, :, 0:256:ZC].rearrange("p r (b t) -> p r b t", b=2)
        centring = sem("centring")

        def tiles_of(ap):
            return ap.rearrange("p (t k) -> p t k", t=KT)

        def flat_of(ap):
            return ap.rearrange("p n x -> p (n x)")

        def lab_of(n):
            return lab[:, :, :].rearrange("p (r b n) t -> p r b n t", b=2, n=NSEQ)[:, :, :, n, :]

        def down_at(n):
            return down[:, :, bass.ds(n * NMEM, NMEM)].rearrange("p w (g r) -> p w g r", g=2)

        block = ctx.enter_context(nc.Block())

        @block.sync
        def _(sp):
            sp.dma_start(ident[:, :], c_ident).then_inc(const_in, 16)
            sp.dma_start(sel[:, :], c_sel).then_inc(const_in, 16)
            sp.dma_start(tempc[:, :], temp.rearrange("(o t) -> o t", o=1).broadcast_to((P, 1))).then_inc(const_in, 16)
            sp.dma_start(te_raw[:, :, :], te_v[0]).then_inc(te_in, 16)
            for b in range(BATCHES):
                if b:
                    sp.wait_ge(lab_sum, 2 * b)
                sp.dma_start(lab_raw, lab_v[b * IMG:(b + 1) * IMG, :, 1:3, :]).then_inc(lab_in, 16)
            sp.wait_ge(lab_sum, 2 * BATCHES)
            for u in range(U):
                sp.dma_start(raw[u], tr_v[u, 0]).then_inc(tr_in[u], 16)

            def refill(q, m, n, u):
                sp.wait_ge(squared, q - U + 1)
                sp.wait_ge(rounded, q - U + 1)
                sp.wait_ge(rest, q - U + 1)
                sp.dma_start(raw[u], tr_v[m, n]).then_inc(tr_in[u], 16)

            def bodies(n, i0):
                with sp.Fori(i0, BODIES) as i:
                    for u in range(U):
                        refill(n * NMEM + i * U + u, i * U + u, n, u)

            bodies(0, 1)
            with sp.Fori(1, NSEQ) as n:
                sp.wait_ge(te_scaled, n * CC)
                sp.dma_start(te_raw[:, :, :], te_v[n]).then_inc(te_in, 16)
                bodies(n, 0)
            for u in range(AHEAD):
                refill(PAIRS + u, u, 0, u)
            sp.wait_ge(squared, PAIRS + AHEAD)
            sp.wait_ge(rounded, PAIRS + AHEAD)
            sp.wait_ge(rest, PAIRS + AHEAD)
            sp.dma_start(up32, c_up.rearrange("p (v y) -> p v y", v=VAR)).then_inc(x_in, 16)
            sp.dma_start(xin, x.rearrange("o n y x -> y (o n) x")).then_inc(x_in, 16)
            sp.wait_ge(tail, 4)
            sp.dma_start(out.rearrange("o n y x -> y (o n) x"), var).then_inc(out_done, 16)
            sp.wait_ge(out_done, 16)

        @block.scalar
        def _(act):
            act.sem_inc(exped, KT)

            def prepare(q, s, loads, late=True):
                act.wait_ge(tr_in[s], loads * 16)
                if late or q >= 2:
                    act.wait_ge(added, q - 1)
                act.activation(sq[s % 2][:, :, :], raw[s], ACT.Square).then_inc(squared, 1)
                if late:
                    act.wait_ge(scored, (q - U + 2) * KT)
                act.copy(hi[s][:, :, :], raw[s]).then_inc(rounded, 1)

            def exps(q, duo, u, tiles):
                if 0 in tiles:
                    act.wait_ge(root, (duo + 1) * RSQ)
                    act.wait_ge(weighed, q + 1)
                for t in tiles:
                    act.wait_ge(scored, q * KT + (KT + t + 1))
                    act.activation(prob[u % 2][:, t, :], s_bank[t][0:KP, 0:PIX], ACT.Exp,
                                   scale=rk[u // 2][0:KP, (u % 2) * KT + t:(u % 2) * KT + t + 1]).then_inc(exped, 1)

            for q in range(AHEAD):
                prepare(q, q, 1, late=False)
            with act.Fori(0, NSEQ) as n:
                act.wait_ge(te_in, n * 16 + 16)
                act.wait_ge(te_ready, n + 1)
                act.activation(te_sq[:, :, :], te_raw[:, :, :], ACT.Square).then_inc(te_squared, 1)
                act.wait_ge(te_scaled, n * CC + CC)
                act.wait_ge(scored, n * (NMEM * KT) + KT)
                act.copy(te_hi[:, :, :], te_sq[:, :, :]).then_inc(te_rounded, 1)
                with act.Fori(0, BODIES) as i:
                    for u in range(U):
                        q = n * NMEM + i * U + u
                        duo = n * (NMEM // 2) + i * (U // 2) + u // 2
                        exps(q, duo, u, (0, 1))
                        prepare(q + AHEAD, (u + AHEAD) % U, n * BODIES + i + ((u + AHEAD) // U + 1))
                        exps(q, duo, u, (2, 3))

            def read_up(j, x):
                act.wait_ge(upped, j + 1)
                if not (isinstance(j, int) and j < 2):
                    act.wait_ge(up_reduced, j - 1)
                k = x if isinstance(x, int) else (x[1])
                at = x if isinstance(x, int) else x[0]
                act.activation(up_sq[k % 2], s_bank[k % 4][0:WL, 0:PAIRS], ACT.Square).then_inc(up_squared, 1)
                act.copy(mean[:, :, at], s_bank[k % 4][0:WL, PAIRS:PAIRS + NSEQ]).then_inc(up_read, 1)

            act.wait_ge(x_in, 32)
            act.copy(up[:, :, :], up32).then_inc(centred, 1)
            act.sem_inc(up_read, 4)
            act.wait_ge(weighed, PAIRS + 2)
            for j in (0, 1):
                read_up(j, j)
            with act.Fori(0, 5) as w:
                for k in range(16):
                    j = w * 16 + (2 + k)
                    read_up(j, (j, 2 + k))
            for j in range(82, WL):
                read_up(j, j)
            act.wait_ge(tail, 2)
            act.activation(xm[:, :], xm[:, :], ACT.Exp, scale=ALPHA, bias=bias[0:WL, 0:1]).then_inc(tail_exp, 1)

        @block.gpsimd
        def _(pool):
            pool.memset(ones[:, :], 1.0).then_inc(inited, 1)
            pool.memset(z_all[:, :], 0.0).then_inc(inited, 1)
            pool.memset(zeros[:, :], 0.0).then_inc(inited, 1)
            pool.memset(bias[:, :], -ALPHA).then_inc(inited, 1)
            for s in range(2):
                pool.memset(sumsq[s][:, :, :], 1.0).then_inc(inited, 1)
            pool.wait_ge(inited, 2)
            pool.memset(z_rows[:, :, 1:257:ZC], 1.0).then_inc(inited, 1)
            pool.sem_inc(z_ready, 1)
            with pool.Fori(0, NSEQ) as n:
                with pool.Fori(0, BODIES) as i:
                    pool.wait_ge(z_built, n + 1)
                    for u in range(U):
                        pool.wait_ge(weighed, n * NMEM + i * U + (u + 1))
                        pool.tensor_copy(z[u % 2][:, :], z_all[:, bass.ds((i * U + u) * (KT * ZC), KT * ZC)]).then_inc(z_ready, 1)

        @block.vector
        def _(dve):
            def newton(r, a, b, square, out, s, base):
                bits = r.bitcast(I32)
                dve.tensor_scalar(bits, square.bitcast(I32), 1, None, ALU.arith_shift_right).then_inc(s, 1)
                dve.wait_ge(s, base + 1)
                dve.tensor_scalar(bits, bits, -1.0, float(MAGIC), ALU.mult, ALU.add).then_inc(s, 1)
                for k in range(STEPS):
                    at = base + 2 + 3 * k
                    dve.wait_ge(s, at)
                    dve.tensor_tensor(a, r, r, ALU.mult).then_inc(s, 1)
                    dve.wait_ge(s, at + 1)
                    dve.scalar_tensor_tensor(out=b, in0=a, scalar=-0.5, in1=square, op0=ALU.mult, op1=ALU.mult).then_inc(s, 1)
                    dve.wait_ge(s, at + 2)
                    dve.scalar_tensor_tensor(out=out if k == STEPS - 1 else r, in0=b, scalar=1.5, in1=r,
                                             op0=ALU.add, op1=ALU.mult).then_inc(s, 1)

            def prepare(q, s, late=True):
                dve.wait_ge(squared, q + 1)
                if late or q >= 2:
                    dve.wait_ge(normed, q - 1)
                dve.tensor_tensor(sumsq[s % 2][:, :, 0:KP], tiles_of(sq[s % 2][:, 0, :]), tiles_of(sq[s % 2][:, 1, :]),
                                  ALU.add).then_inc(added, 1)
                dve.wait_ge(rounded, q + 1)
                dve.tensor_tensor(lo[s][:, :, :], raw[s], hi[s][:, :, :].bitcast(F32), ALU.subtract).then_inc(rest, 1)

            def roots(duo, s, late=True):
                dve.wait_ge(normed, duo * 2 + 2)
                dve.transpose(norms[:, :, :].rearrange("p a b -> p (a b)"), n_bank[:, 0:2 * P]).then_inc(root, 1)
                dve.wait_ge(root, duo * RSQ + 1)
                if late:
                    dve.wait_ge(exped, (duo - U // 2) * (2 * KT) + (2 * KT + KT))
                newton(seed[:, :], root_a[:, :], root_b[:, :], norms[:, :, 0], rk[s][:, :], root, duo * RSQ + 1)

            dve.sem_inc(te_ready, 1)
            dve.sem_inc(kept, 2)
            dve.sem_inc(divided, 2)
            for b in range(BATCHES):
                dve.wait_ge(lab_in, 16 * b + 16)
                mid = lab_raw.rearrange("p y r (x q) -> p y r x q", q=UPS)
                dve.tensor_tensor(lab_rows[:, :, :, :], mid[:, :, 0, :, 1:3], mid[:, :, 1, :, 1:3], ALU.add).then_inc(lab_sum, 1)
                dve.wait_ge(lab_sum, 2 * b + 1)
                if b:
                    dve.wait_ge(lab_turned, KT * b)
                dve.tensor_tensor(lab_down[:, :].rearrange("p (y x) -> p y x", y=WF), lab_rows[:, :, :, 0], lab_rows[:, :, :, 1],
                                  ALU.add).then_inc(lab_sum, 1)
                for t in range(KT):
                    dve.wait_ge(lab_turned, KT * b + t + 1)
                    dve.tensor_scalar(lab[:, b * IMG:(b + 1) * IMG, t], s_bank[t][0:KP, 0:IMG], 0.25, None,
                                      ALU.mult).then_inc(lab_kept, 1)
            dve.wait_ge(inited, 7)
            dve.wait_ge(const_in, 48)
            for q in range(AHEAD):
                prepare(q, q, late=False)
                if q % 2:
                    roots(q // 2, q // 2, late=False)
            dve.wait_ge(lab_kept, BATCHES * KT)
            with dve.Fori(0, NSEQ) as n:
                dve.wait_ge(z_ready, n * NMEM + 1)
                dve.tensor_copy(z_labels, lab_of(n)).then_inc(z_built, 1)
                dve.wait_ge(te_squared, n + 1)
                dve.tensor_tensor(te_ss[:, :], te_sq[:, 0, :], te_sq[:, 1, :], ALU.add).then_inc(te_added, 1)
                dve.wait_ge(te_summed, n + 1)
                newton(te_r[:, :], te_a[:, :], te_b[:, :], m_bank[:, 0:PIX], te_r[:, :], te_root, n * (RSQ - 1))
                dve.wait_ge(te_root, n * (RSQ - 1) + (RSQ - 1))
                for c in range(CC):
                    dve.scalar_tensor_tensor(out=te_sq[:, c, :].rearrange("p (x y) -> p x y", x=HF),
                                             in0=te_raw[:, c, :].rearrange("p (y x) -> p x y", y=WF),
                                             scalar=tempc[:, 0:1],
                                             in1=te_r[:, :].rearrange("p (y x) -> p x y", y=WF),
                                             op0=ALU.mult, op1=ALU.mult).then_inc(te_scaled, 1)
                dve.wait_ge(te_rounded, n + 1)
                dve.tensor_tensor(te_lo[:, :, :], te_sq[:, :, :], te_hi[:, :, :].bitcast(F32), ALU.subtract).then_inc(te_ready, 1)
                with dve.Fori(0, BODIES) as i:
                    for u in range(U):
                        v = u + AHEAD
                        prepare(n * NMEM + i * U + v, v % U)
                        if v % 2:
                            roots(n * (NMEM // 2) + i * (U // 2) + v // 2, v % U // 2)
                dve.wait_ge(weighed, n * NMEM + (NMEM + 2))
                dve.wait_ge(gathered, n + 1)
                for g in range(2):
                    dve.tensor_copy(sums[g][:, :], pv_bank[g][:, 0:PIX]).then_inc(kept, 1)
                dve.wait_ge(gathered, n + 2)
                quot = m_bank[0:WP, 0:12 * ZC].rearrange("p (w g d r) -> p w g d r", w=6, g=2, d=2)
                dve.reciprocal(rden[:, :, :, :], quot[:, :, :, 1, 0:ROWS]).then_inc(divided, 1)
                dve.wait_ge(divided, n * 2 + 3)
                dve.tensor_tensor(down_at(n), quot[:, :, :, 0, 0:ROWS], rden[:, :, :, :], ALU.mult).then_inc(divided, 1)

            dve.wait_ge(divided, 2 * NSEQ + 2)
            down4 = down[:, :, 0:PAIRS].rearrange("p w (n m) -> p w n m", m=NMEM)
            for w in range(6):
                dve.tensor_reduce(down[:, w, PAIRS:], down4[:, w], AX.X, ALU.add).then_inc(centring, 1)
            dve.wait_ge(centring, 6)
            dve.tensor_scalar(down[:, :, PAIRS:], down[:, :, PAIRS:], 1.0 / NMEM, None, ALU.mult).then_inc(centring, 1)
            dve.wait_ge(centring, 7)
            for w in range(6):
                dve.tensor_tensor(down4[:, w], down4[:, w],
                                  down[:, w, PAIRS:].rearrange("p (n o) -> p n o", o=1).broadcast_to((WP, NSEQ, NMEM)), ALU.subtract).then_inc(centring, 1)
            dve.wait_ge(centring, 13)
            dve.tensor_copy(down_hi[:, :, :], down[:, :, :]).then_inc(centring, 1)
            dve.wait_ge(centring, 14)
            dve.tensor_tensor(down_lo[:, :, :], down[:, :, :], down_hi[:, :, :].bitcast(F32), ALU.subtract).then_inc(centring, 1)

            def reduce(j, k, x):
                dve.wait_ge(up_squared, j + 1)
                dve.tensor_reduce(var[:, :, x], up_sq[k % 2].rearrange("p (n m) -> p n m", m=NMEM), AX.X,
                                  ALU.add).then_inc(up_reduced, 1)

            for j in (0, 1):
                reduce(j, j, j)
            with dve.Fori(0, 5) as w:
                for k in range(16):
                    reduce(w * 16 + (2 + k), 2 + k, w * 16 + (2 + k))
            for j in range(82, WL):
                reduce(j, j, j)
            dve.wait_ge(up_reduced, WL)
            dve.tensor_scalar(xm[:, :], flat_of(var), 1.0 / (NMEM - 1), 1.0, ALU.mult, ALU.add).then_inc(tail, 1)
            dve.wait_ge(tail, 1)
            dve.reciprocal(xm[:, :], xm[:, :]).then_inc(tail, 1)
            dve.wait_ge(tail_exp, 1)
            dve.wait_ge(up_read, WL + 4)
            dve.tensor_tensor(xm[:, :], xm[:, :], flat_of(mean), ALU.mult).then_inc(tail, 1)
            dve.wait_ge(tail, 3)
            dve.tensor_tensor(flat_of(var), xm[:, :], flat_of(xin), ALU.add).then_inc(tail, 1)

        @block.tensor
        def _(pe):
            pe.sem_inc(weighed, 2)
            pe.sem_inc(scored, KT)
            pe.sem_inc(gathered, 1)

            def norm(q, s, duo):
                pe.wait_ge(added, q + 1)
                if s % 2 == 0 and not (isinstance(duo, int) and duo == 0):
                    pe.wait_ge(root, (duo - 1) * RSQ + 1)
                at = s % 2 * P
                for g in range(4):
                    mm = pe.matmul(n_bank[32 * g:32 * g + 32, at:at + P], ones[:, 0:32], sumsq[s % 2][:, :, 32 * g:32 * g + 32],
                                   start=True, stop=True)
                mm.then_inc(normed, 1)

            def scores(q, s, t):
                if t == 0:
                    pe.wait_ge(rest, q + 1)
                pe.wait_ge(exped, q * KT + (t + 1))
                for k, (part, c, te) in enumerate([(hi, 0, te_hi), (hi, 0, te_lo), (hi, 1, te_hi), (hi, 1, te_lo),
                                                   (lo, 0, te_hi), (lo, 1, te_hi)]):
                    mm = pe.matmul(s_bank[t][0:KP, 0:PIX], part[s][:, c, t * KP:(t + 1) * KP], te[:, c, :],
                                   start=(k == 0), stop=(k == 5))
                mm.then_inc(scored, 1)

            def weigh(q, u):
                pe.wait_ge(z_ready, q + 2)
                pe.wait_ge(exped, q * KT + 2 * KT)
                for t in range(KT):
                    mm = pe.matmul(pv_bank[u % 2][32 * t:32 * t + 32, 0:PIX], z[u % 2][:, t * ZC:(t + 1) * ZC], prob[u % 2][:, t, :],
                                   start=False, stop=False, skip_group_check=True)
                mm.then_inc(weighed, 1)

            pe.wait_ge(const_in, 48)
            for b in range(BATCHES):
                pe.wait_ge(lab_sum, 2 * b + 2)
                for t in range(KT):
                    if b:
                        pe.wait_ge(lab_kept, KT * (b - 1) + t + 1)
                    pe.transpose(s_bank[t][0:KP, 0:IMG], lab_down[:, t * KP:(t + 1) * KP], ident[0:IMG, 0:IMG]).then_inc(lab_turned, 1)
            pe.wait_ge(lab_kept, BATCHES * KT)
            pe.wait_ge(inited, 7)
            for q in range(AHEAD):
                norm(q, q, q // 2)
            with pe.Fori(0, NSEQ) as n:
                pe.wait_ge(kept, n * 2 + 2)
                for g in range(2):
                    for t in range(KT):
                        pe.matmul(pv_bank[g][32 * t:32 * t + 32, 0:PIX], zeros[0:KP, 0:32], zeros[0:KP, 0:PIX],
                                  start=True, stop=False, skip_group_check=True)
                pe.wait_ge(te_added, n + 1)
                pe.wait_ge(divided, n * 2 + 2)
                pe.matmul(m_bank[:, 0:PIX], ones[:, :], te_ss[:, :], start=True, stop=True).then_inc(te_summed, 1)
                with pe.Fori(0, BODIES) as i:
                    pe.wait_ge(te_ready, n + 2)
                    for u in range(U):
                        q = n * NMEM + i * U + u
                        scores(q, u, 0)
                        scores(q, u, 1)
                        if u:
                            weigh(n * NMEM + i * U + (u - 1), u - 1)
                        scores(q, u, 2)
                        scores(q, u, 3)
                        v = u + AHEAD
                        norm(n * NMEM + i * U + v, v % U, n * (NMEM // 2) + i * (U // 2) + v // 2)
                    weigh(n * NMEM + i * U + (U - 1), U - 1)
                pe.wait_ge(kept, n * 2 + 4)
                for w in range(6):
                    for g in range(2):
                        at = (2 * w + g) * ZC
                        mm = pe.matmul(m_bank[0:WP, at:at + ZC], sums[g][:, WINDOWS[w] * WF:WINDOWS[w] * WF + WP], sel[:, :],
                                       start=True, stop=True)
                mm.then_inc(gathered, 1)

            def upsample(j, b, k, hi_w, lo_w):
                pe.wait_ge(up_read, j + 1)
                pe.matmul(s_bank[b][0:WL, 0:NCOL], up[:, k, :], hi_w, start=True, stop=False)
                pe.matmul(s_bank[b][0:WL, 0:NCOL], up[:, k, :], lo_w, start=False, stop=True).then_inc(upped, 1)

            pe.wait_ge(exped, PAIRS * KT + KT)
            pe.wait_ge(centred, 1)
            pe.wait_ge(centring, 15)
            for j in (0, 1):
                upsample(j, j % 4, 16, down_hi[:, 0, :], down_lo[:, 0, :])
            with pe.Fori(0, 5) as w:
                for k in range(16):
                    upsample(w * 16 + (2 + k), (2 + k) % 4, k, down_hi[:, w, :], down_lo[:, w, :])
            for j in range(82, WL):
                upsample(j, j % 4, j - 82 + 12 if j < 86 else 17, down_hi[:, 5, :], down_lo[:, 5, :])


_INS = ["x", "L0_conv_train_labels", "L0_conv_test_feat", "L0_conv_train_feats", "L0_conv_softmax_temp"]


def kernel(**inputs):
    import numpy as np
    import concourse.bacc as bacc
    from concourse.bass_utils import run_bass_kernel_spmd

    nc = bacc.Bacc("TRN2", target_bir_lowering=False, num_devices=1)
    arrays = {name: np.ascontiguousarray(inputs[name]) for name in _INS}
    arrays |= {"c_ident": np.eye(P, dtype=np.float32), "c_sel": selector(), "c_up": upsampling()}
    args = [nc.dram_tensor(name, a.shape, mybir.dt.from_np(a.dtype), kind="ExternalInput").ap() for name, a in arrays.items()]
    out = nc.dram_tensor("out", (1, NSEQ, WL, HL), F32, kind="ExternalOutput").ap()
    build(nc, *args, out)
    r = run_bass_kernel_spmd(nc, [arrays], core_ids=[0])
    return r.results[0]["out"]
```

```python
from contextlib import ExitStack

import concourse.bass as bass
from concourse import mybir

ALU = mybir.AluOpType
ACT = mybir.ActivationFunctionType
AX = mybir.AxisListType
F32 = mybir.dt.float32
F32R = mybir.dt.float32r
I32 = mybir.dt.int32
BF16 = mybir.dt.bfloat16

P = 128
NMEM, NSEQ, C, WF, HF = 30, 16, 256, 22, 22
WL, HL = 88, 88
PIX = WF * HF
CC = C // P
KT = 4
KP = PIX // KT
ZC = 32
U = 6
BODIES = NMEM // U
PAIRS = NMEM * NSEQ
SLOT = NMEM + 1
NCOL = NSEQ * SLOT
COLS = 32 + NCOL
DIV = 7
AHEAD = U - 1
ROWS = NMEM // 2
WIN = 5
WP = WIN * WF
WINDOWS = [4 * w for w in range(5)] + [HF - WIN]
UPS = 4
VAR = 16 + 2
ALPHA = 20.0
STEPS = 3
RSQ = 3 + 3 * STEPS
MAGIC = 0x5F3759DF


def upsampling():
    import numpy as np

    def line(n_in, n_out):
        w = np.zeros((n_in, n_out), np.float32)
        for o in range(n_out):
            at = (o + 0.5) * n_in / n_out - 0.5
            lo = int(np.floor(at))
            for i, f in ((lo, 1 - (at - lo)), (lo + 1, at - lo)):
                w[min(max(i, 0), n_in - 1), o] += f
        return w

    rows = line(WF, WL)
    up = np.zeros((WIN, WF, VAR, WL), np.float32)
    for k in range(16):
        v, f = k // UPS, (k % UPS + 0.5) / UPS
        up[v, :, k] = (1 - f) * rows
        up[v + 1, :, k] = f * rows
    up[0, :, 16] = rows
    up[WIN - 1, :, 17] = rows
    return up.reshape(WP, VAR * WL)


def selector():
    import numpy as np

    s = np.zeros((KT, ZC // 2, 2, 2, ZC // 2), np.float32)
    for r in range(ZC // 2):
        for d in range(2):
            s[:, r, d, d, r] = 1.0
    return s.reshape(P, ZC)


GROUPS = 22


def groups(eng, work):
    with eng.Fori(0, 5) as w:
        for v in range(4):
            work(w * 4 + v, v % 2, [(0, w * 16 + (2 + 4 * v), 4)])
    work(20, 0, [(0, 82, 4)])
    work(21, 1, [(0, 0, 2), (2, 86, 2)])


def build(nc, x, labels, test_feat, train_feats, temp, c_ident, c_sel, c_up, out):
    with ExitStack() as ctx:
        def sb(name, shape, dt=F32):
            return ctx.enter_context(nc.sbuf_tensor(name, shape, dt))

        def sem(name):
            return ctx.enter_context(nc.semaphore(name))

        raw_all = sb("raw_all", [P, U, CC, PIX])
        raw = [raw_all[:, s] for s in range(U)]
        hi = [sb(f"hi{s}", [P, CC, PIX], F32R) for s in range(U)]
        lo = [sb(f"lo{s}", [P, CC, PIX], F32R) for s in range(U)]
        sq = [sb(f"sq{s}", [P, CC, PIX]) for s in range(2)]
        sumsq = [sb(f"sumsq{s}", [P, 2, KT, P]) for s in range(U // 2)]
        norms = sb("norms", [P, 2 * KT, 32])
        seed = sb("seed", [P, 2 * KT])
        root_a = sb("root_a", [P, 2 * KT])
        root_b = sb("root_b", [P, 2 * KT])
        rk = [sb(f"rk{s}", [P, 2 * KT]) for s in range(U // 2)]
        prob = [sb(f"prob{s}", [KP, KT, PIX]) for s in range(2)]
        z_all = sb("z_all", [KP, ROWS * 258])
        z_rows = z_all[:, :].rearrange("p (r x) -> p r x", r=ROWS)
        z_labels = z_rows[:, :, 0:256:ZC].rearrange("p r (b t) -> p r b t", b=2)
        z = [sb(f"z{s}", [KP, KT * ZC]) for s in range(2)]
        lab_raw = sb("lab_raw", [NMEM, WF, 2, HL])
        lab_rows = sb("lab_rows", [NMEM, WF, HF, 2])
        lab_down = sb("lab_down", [NMEM, PIX])
        lab = sb("lab", [KP, NMEM, KT])
        te_raw = sb("te_raw", [P, CC, PIX])
        te_sq = sb("te_sq", [P, CC, PIX])
        te_ss = sb("te_ss", [P, KT, P])
        te_norms = sb("te_norms", [P, KT, 32])
        te_rk = sb("te_rk", [P, KT])
        te_diag = sb("te_diag", [KP, KT, KP])
        te_hi = sb("te_hi", [P, 2 * CC * PIX], F32R)
        te_lo = sb("te_lo", [P, 2 * CC * PIX], F32R)
        sums = [sb(f"sums{g}", [P, PIX]) for g in range(2)]
        rden = sb("rden", [WP, 6, 2, ROWS])
        dev = sb("dev", [WP, 6, SLOT])
        dsum = sb("dsum", [WP, 6])
        down_hi = sb("down_hi", [WP, 6, COLS], F32R)
        down_lo = sb("down_lo", [WP, 6, COLS], F32R)
        up = sb("up", [WP, VAR, WL], F32R)
        ident = sb("ident", [P, P])
        ones = sb("ones", [P, P])
        sel = sb("sel", [P, ZC])
        tempc = sb("tempc", [P, 1])
        zeros = sb("zeros", [P, 512], BF16)
        bias = sb("bias", [P, 1])

        flat = raw_all[:, :, :, :].rearrange("p u c k -> p (u c k)")
        up32 = flat[0:WP, 0:VAR * WL].rearrange("p (v y) -> p v y", v=VAR)
        at = VAR * WL
        xin, mean, var = (
            flat[0:WL, at + NSEQ * HL * b:at + NSEQ * HL * (b + 1)].rearrange("p (n x) -> p n x", x=HL)
            for b in range(3)
        )
        xm = z_all[0:WL, 0:NSEQ * HL]
        up_sq = [prob[b][0:WL, :, 0:PAIRS].rearrange("p j (n m) -> p j n m", m=NMEM) for b in range(2)]

        psum = [ctx.enter_context(nc.psum_tensor(f"banks{h}", [P, 4, 512], F32)) for h in range(2)]
        s_bank = [psum[0][:, t] for t in range(KT)]
        n_bank, pv_bank, m_bank = psum[1][:, 0], (psum[1][:, 1], psum[1][:, 2]), psum[1][:, 3]

        const_in, lab_in, te_in, x_in = sem("const_in"), sem("lab_in"), sem("te_in"), sem("x_in")
        tr_in = [sem(f"tr_in{s}") for s in range(U)]
        inited = sem("inited")
        lab_sum, lab_turned, lab_kept = sem("lab_sum"), sem("lab_turned"), sem("lab_kept")
        squared, rounded, rest, added = sem("squared"), sem("rounded"), sem("rest"), sem("added")
        normed, root = sem("normed"), sem("root")
        scored, exped, z_built, z_ready, weighed = (sem(k) for k in ("scored", "exped", "z_built", "z_ready", "weighed"))
        kept, gathered, divided = sem("kept"), sem("gathered"), sem("divided")
        te_squared, te_added, te_normed, te_diaged, te_spread = (
            sem(k) for k in ("te_squared", "te_added", "te_normed", "te_diaged", "te_spread"))
        te_root, te_scaled, te_rounded, te_ready = (sem(k) for k in ("te_root", "te_scaled", "te_rounded", "te_ready"))
        up_ready, upped, up_squared, up_read, up_reduced = (
            sem(k) for k in ("up_ready", "upped", "up_squared", "up_read", "up_reduced"))
        tail, tail_exp, out_done = sem("tail"), sem("tail_exp"), sem("out_done")

        tr_v = train_feats.rearrange("m n (p c) h w -> m n p c (h w)", c=CC)
        te_v = test_feat.rearrange("o n (p c) h w -> (o n) p c (h w)", c=CC)
        lab_v = labels.rearrange("m n (y r) x -> n m y r x", r=UPS)

        def tiles_of(ap):
            return ap.rearrange("p (t k) -> p t k", t=KT)

        def flat_of(ap):
            return ap.rearrange("p n x -> p (n x)")

        def te_part(part, n, c):
            return part[:, bass.ds(n % 2 * (CC * PIX) + c * PIX, PIX)]

        block = ctx.enter_context(nc.Block())

        @block.sync
        def _(sp):
            def next_test(n):
                sp.dma_start(te_raw[:, :, :], te_v[n]).then_inc(te_in, 16)
                sp.dma_start(lab_raw[:, :, :, :], lab_v[n, :, :, 1:3, :]).then_inc(lab_in, 16)

            sp.dma_start(te_raw[:, :, :], te_v[0]).then_inc(te_in, 16)
            for u in range(2):
                sp.dma_start(raw[u], tr_v[u, 0]).then_inc(tr_in[u], 16)
            sp.dma_start(ident[:, :], c_ident).then_inc(const_in, 16)
            sp.dma_start(sel[:, :], c_sel).then_inc(const_in, 16)
            sp.dma_start(tempc[:, :], temp.rearrange("(o t) -> o t", o=1).broadcast_to((P, 1))).then_inc(const_in, 16)
            sp.dma_start(lab_raw[:, :, :, :], lab_v[0, :, :, 1:3, :]).then_inc(lab_in, 16)
            for u in range(2, U):
                sp.dma_start(raw[u], tr_v[u, 0]).then_inc(tr_in[u], 16)

            def refill(q, m, n, u):
                sp.wait_ge(squared, q - U + 1)
                sp.wait_ge(rounded, q - U + 1)
                sp.wait_ge(rest, q - U + 1)
                sp.dma_start(raw[u], tr_v[m, n]).then_inc(tr_in[u], 16)

            def bodies(n, i0):
                with sp.Fori(i0, BODIES) as i:
                    for u in range(U):
                        refill(n * NMEM + i * U + u, i * U + u, n, u)

            def test_free(n):
                sp.wait_ge(te_scaled, n * CC)
                sp.wait_ge(lab_sum, n * 2)

            test_free(1)
            next_test(1)
            bodies(0, 1)
            with sp.Fori(1, NSEQ - 1) as n:
                test_free(n + 1)
                next_test(n + 1)
                bodies(n, 0)
            test_free(NSEQ)
            next_test(0)
            bodies(NSEQ - 1, 0)
            for u in range(AHEAD):
                refill(PAIRS + u, u, 0, u)
            sp.wait_ge(squared, PAIRS + AHEAD)
            sp.wait_ge(rounded, PAIRS + AHEAD)
            sp.wait_ge(rest, PAIRS + AHEAD)
            sp.dma_start(up32, c_up.rearrange("p (v y) -> p v y", v=VAR)).then_inc(x_in, 16)
            sp.dma_start(xin, x.rearrange("o n y x -> y (o n) x")).then_inc(x_in, 16)
            sp.wait_ge(tail, 4)
            sp.dma_start(out.rearrange("o n y x -> y (o n) x"), var).then_inc(out_done, 16)
            sp.wait_ge(out_done, 16)

        @block.scalar
        def _(act):
            act.sem_inc(exped, KT)

            def prepare(q, s, loads, late=True):
                act.wait_ge(tr_in[s], loads * 16)
                if late or q >= 2:
                    act.wait_ge(added, q - 1)
                act.activation(sq[s % 2][:, :, :], raw[s], ACT.Square).then_inc(squared, 1)
                if late:
                    act.wait_ge(scored, (q - U + 2) * KT)
                act.copy(hi[s][:, :, :], raw[s]).then_inc(rounded, 1)

            def exps(q, duo, u, tiles):
                if 0 in tiles:
                    act.wait_ge(root, (duo + 1) * RSQ)
                    act.wait_ge(weighed, q + 1)
                for t in tiles:
                    act.wait_ge(scored, q * KT + (KT + t + 1))
                    act.activation(prob[u % 2][:, t, :], s_bank[t][0:KP, 0:PIX], ACT.Exp,
                                   scale=rk[u // 2][0:KP, (u % 2) * KT + t:(u % 2) * KT + t + 1]).then_inc(exped, 1)

            def square_test(n):
                act.wait_ge(te_in, n * 16 + 16)
                act.activation(te_sq[:, :, :], te_raw[:, :, :], ACT.Square).then_inc(te_squared, 1)

            def body(n, i, first):
                for u in range(U):
                    q = n * NMEM + i * U + u
                    duo = n * (NMEM // 2) + i * (U // 2) + u // 2
                    exps(q, duo, u, (0, 1))
                    prepare(q + AHEAD, (u + AHEAD) % U, n * BODIES + i + ((u + AHEAD) // U + 1))
                    exps(q, duo, u, (2, 3))
                    if first and u == 0:
                        act.wait_ge(te_ready, n + 1)
                        square_test(n + 1)

            square_test(0)
            for q in range(AHEAD):
                prepare(q, q, 1, late=False)
            with act.Fori(0, NSEQ) as n:
                body(n, 0, first=True)
                with act.Fori(1, BODIES) as i:
                    body(n, i, first=False)

            def read_up(g, h, pieces):
                act.wait_ge(upped, g + 1)
                act.wait_ge(up_reduced, g + 1)
                cols = psum[h][0:WL, :, 0:NCOL].rearrange("p j (n m) -> p j n m", m=SLOT)
                act.activation(up_sq[h], cols[:, :, :, 0:NMEM], ACT.Square).then_inc(up_squared, 1)
                for j0, x0, k in pieces:
                    last = act.copy(mean[:, :, bass.ds(x0, k)].rearrange("p n x -> p x n"), cols[:, j0:j0 + k, :, NMEM])
                last.then_inc(up_read, 1)

            act.wait_ge(x_in, 32)
            act.copy(up[:, :, :], up32).then_inc(up_ready, 1)
            act.sem_inc(up_read, 2)
            act.wait_ge(weighed, PAIRS + 2)
            groups(act, read_up)
            act.wait_ge(tail, 2)
            act.activation(xm, xm, ACT.Exp, scale=ALPHA, bias=bias[0:WL, 0:1]).then_inc(tail_exp, 1)

        @block.gpsimd
        def _(pool):
            pool.memset(ones[:, :], 1.0).then_inc(inited, 1)
            for s in range(U // 2):
                pool.memset(sumsq[s][:, :, :, :], 1.0).then_inc(inited, 1)
            pool.memset(te_ss[:, :, :], 1.0).then_inc(inited, 1)
            pool.memset(zeros[:, :], 0.0).then_inc(inited, 1)
            for g in range(2):
                pool.memset(sums[g][:, :], 1.0).then_inc(inited, 1)
            pool.memset(z_all[:, :], 0.0).then_inc(inited, 1)
            pool.memset(bias[:, :], -ALPHA).then_inc(inited, 1)
            pool.wait_ge(inited, 10)
            pool.memset(z_rows[:, :, 1:257:ZC], 1.0).then_inc(inited, 1)
            pool.sem_inc(z_ready, 1)
            with pool.Fori(0, NSEQ) as n:
                with pool.Fori(0, BODIES) as i:
                    pool.wait_ge(z_built, n + 1)
                    for u in range(U):
                        pool.wait_ge(weighed, n * NMEM + i * U + (u + 1))
                        pool.tensor_copy(z[u % 2][:, :], z_all[:, bass.ds((i * U + u) * (KT * ZC), KT * ZC)]).then_inc(z_ready, 1)

        @block.vector
        def _(dve):
            def newton(r, a, b, square, out, s, base):
                bits = r.bitcast(I32)
                dve.tensor_scalar(bits, square.bitcast(I32), 1, None, ALU.arith_shift_right).then_inc(s, 1)
                dve.wait_ge(s, base + 1)
                dve.tensor_scalar(bits, bits, -1.0, float(MAGIC), ALU.mult, ALU.add).then_inc(s, 1)
                for k in range(STEPS):
                    at = base + (2 + 3 * k)
                    dve.wait_ge(s, at)
                    dve.tensor_tensor(a, r, r, ALU.mult).then_inc(s, 1)
                    dve.wait_ge(s, at + 1)
                    dve.scalar_tensor_tensor(out=b, in0=a, scalar=-0.5, in1=square, op0=ALU.mult, op1=ALU.mult).then_inc(s, 1)
                    dve.wait_ge(s, at + 2)
                    dve.scalar_tensor_tensor(out=out if k == STEPS - 1 else r, in0=b, scalar=1.5, in1=r,
                                             op0=ALU.add, op1=ALU.mult).then_inc(s, 1)

            def prepare(q, s, late=True):
                dve.wait_ge(squared, q + 1)
                dve.tensor_tensor(sumsq[s // 2][:, s % 2, :, 0:KP], tiles_of(sq[s % 2][:, 0, :]), tiles_of(sq[s % 2][:, 1, :]),
                                  ALU.add).then_inc(added, 1)
                dve.wait_ge(rounded, q + 1)
                dve.tensor_tensor(lo[s][:, :, :], raw[s], hi[s][:, :, :].bitcast(F32), ALU.subtract).then_inc(rest, 1)

            def roots(duo, s, late=True):
                dve.wait_ge(normed, duo + 1)
                dve.transpose(norms[:, :, :].rearrange("p a b -> p (a b)"), n_bank[:, 0:2 * P]).then_inc(root, 1)
                dve.wait_ge(root, duo * RSQ + 1)
                if late:
                    dve.wait_ge(exped, (duo - U // 2) * (2 * KT) + (2 * KT + KT))
                newton(seed[:, :], root_a[:, :], root_b[:, :], norms[:, :, 0], rk[s][:, :], root, duo * RSQ + 1)

            def add_labels(n):
                dve.wait_ge(lab_in, n * 16 + 16)
                mid = lab_raw[:, :, :, :].rearrange("p y r (x q) -> p y r x q", q=UPS)
                dve.tensor_tensor(lab_rows[:, :, :, :], mid[:, :, 0, :, 1:3], mid[:, :, 1, :, 1:3], ALU.add).then_inc(lab_sum, 1)
                dve.wait_ge(lab_sum, n * 2 + 1)
                dve.tensor_tensor(lab_down[:, :].rearrange("p (y x) -> p y x", y=WF), lab_rows[:, :, :, 0], lab_rows[:, :, :, 1],
                                  ALU.add).then_inc(lab_sum, 1)

            def keep_labels(n):
                dve.wait_ge(lab_turned, n + 1)
                dve.tensor_scalar(lab[:, :, :].rearrange("p m t -> p t m"),
                                  m_bank[0:KP, 0:KT * ZC].rearrange("p (t m) -> p t m", t=KT)[:, :, 0:NMEM], 0.25, None,
                                  ALU.mult).then_inc(lab_kept, 1)

            def add_test(n):
                dve.wait_ge(te_squared, n + 1)
                dve.tensor_tensor(te_ss[:, :, 0:KP], tiles_of(te_sq[:, 0, :]), tiles_of(te_sq[:, 1, :]), ALU.add).then_inc(te_added, 1)

            def root_test(n):
                dve.wait_ge(te_normed, n + 1)
                dve.transpose(te_norms[:, :, :].rearrange("p a b -> p (a b)"), m_bank[:, 0:P]).then_inc(te_root, 1)
                dve.wait_ge(te_root, n * RSQ + 1)
                newton(seed[:, 0:KT], root_a[:, 0:KT], root_b[:, 0:KT], te_norms[:, :, 0], te_rk[:, :], te_root, n * RSQ + 1)
                dve.wait_ge(te_root, n * RSQ + RSQ)
                for t in range(KT):
                    dve.tensor_scalar(te_diag[:, t, :], ident[0:KP, 0:KP], te_rk[0:KP, t:t + 1], None, ALU.mult).then_inc(te_diaged, 1)

            def scale_test(n):
                dve.wait_ge(te_spread, n + 1)
                for c in range(CC):
                    dve.scalar_tensor_tensor(out=te_sq[:, c, :].rearrange("p (x y) -> p x y", x=HF),
                                             in0=te_raw[:, c, :].rearrange("p (y x) -> p x y", y=WF),
                                             scalar=tempc[:, 0:1],
                                             in1=m_bank[:, 0:PIX].rearrange("p (y x) -> p x y", y=WF),
                                             op0=ALU.mult, op1=ALU.mult).then_inc(te_scaled, 1)
                dve.wait_ge(te_scaled, n * CC + CC)
                at = n % 2 * (CC * PIX)
                whole = te_sq[:, :, :].rearrange("p c k -> p (c k)")
                dve.tensor_copy(te_hi[:, bass.ds(at, CC * PIX)], whole).then_inc(te_rounded, 1)
                dve.wait_ge(te_rounded, n + 1)
                dve.tensor_tensor(te_lo[:, bass.ds(at, CC * PIX)], whole, te_hi[:, :].bitcast(F32)[:, bass.ds(at, CC * PIX)],
                                  ALU.subtract).then_inc(te_ready, 1)

            def divide(n):
                dve.wait_ge(gathered, n + 1)
                quot = m_bank[0:WP, 0:12 * ZC].rearrange("p (w g d r) -> p w g d r", w=6, g=2, d=2)
                each = dev[:, :, 0:NMEM]
                dve.reciprocal(rden[:, :, :, :], quot[:, :, :, 1, 0:ROWS]).then_inc(divided, 1)
                dve.wait_ge(divided, n * DIV + 1)
                dve.tensor_tensor(each.rearrange("p w (g r) -> p w g r", g=2), quot[:, :, :, 0, 0:ROWS], rden[:, :, :, :],
                                  ALU.mult).then_inc(divided, 1)
                dve.wait_ge(divided, n * DIV + 2)
                dve.tensor_reduce(dsum[:, :], each, AX.X, ALU.add).then_inc(divided, 1)
                dve.wait_ge(divided, n * DIV + 3)
                dve.tensor_scalar(dev[:, :, NMEM], dsum[:, :], 1.0 / NMEM, None, ALU.mult).then_inc(divided, 1)
                dve.wait_ge(divided, n * DIV + 4)
                dve.tensor_tensor(each, each, dev[:, :, NMEM:SLOT].broadcast_to((WP, 6, NMEM)), ALU.subtract).then_inc(divided, 1)
                dve.wait_ge(divided, n * DIV + 5)
                slot = bass.ds(n * SLOT + 1, SLOT)
                dve.tensor_copy(down_hi[:, :, slot], dev[:, :, :]).then_inc(divided, 1)
                dve.wait_ge(divided, n * DIV + 6)
                dve.tensor_tensor(down_lo[:, :, slot], dev[:, :, :], down_hi[:, :, :].bitcast(F32)[:, :, slot],
                                  ALU.subtract).then_inc(divided, 1)

            def body(n, i, first):
                for u in range(U):
                    if first and u == 0:
                        dve.wait_ge(lab_kept, n + 1)
                        dve.wait_ge(z_ready, n * NMEM + 1)
                        dve.tensor_copy(z_labels, lab[:, :, :].rearrange("p (r b) t -> p r b t", b=2)).then_inc(z_built, 1)
                    if first and u == 1:
                        divide(n)
                        add_labels(n + 1)
                    if first and u == 2:
                        add_test(n + 1)
                    if first and u == 3:
                        dve.wait_ge(z_built, n + 1)
                        keep_labels(n + 1)
                    if first and u == 4:
                        root_test(n + 1)
                    if first and u == 5:
                        scale_test(n + 1)
                    v = u + AHEAD
                    prepare(n * NMEM + i * U + v, v % U)
                    if u % 2:
                        roots(n * (NMEM // 2) + i * (U // 2) + (u + 3) // 2, (u + 3) % U // 2)

            dve.sem_inc(kept, 2)
            dve.wait_ge(inited, 11)
            add_test(0)
            prepare(0, 0, late=False)
            dve.wait_ge(const_in, 48)
            root_test(0)
            prepare(1, 1, late=False)
            roots(0, 0, late=False)
            scale_test(0)
            prepare(2, 2, late=False)
            add_labels(0)
            prepare(3, 3, late=False)
            roots(1, 1, late=False)
            keep_labels(0)
            prepare(4, 4, late=False)
            with dve.Fori(0, NSEQ) as n:
                body(n, 0, first=True)
                with dve.Fori(1, BODIES) as i:
                    body(n, i, first=False)
                dve.wait_ge(weighed, n * NMEM + (NMEM + 2))
                dve.wait_ge(gathered, n + 1)
                for g in range(2):
                    dve.tensor_copy(sums[g][:, :], pv_bank[g][:, 0:PIX]).then_inc(kept, 1)
            divide(NSEQ)

            def reduce(g, h, pieces):
                dve.wait_ge(up_squared, g + 1)
                for j0, x0, k in pieces:
                    last = dve.tensor_reduce(var[:, :, bass.ds(x0, k)].rearrange("p n x -> p x n"), up_sq[h][:, j0:j0 + k], AX.X,
                                             ALU.add)
                last.then_inc(up_reduced, 1)

            dve.sem_inc(up_reduced, 2)
            groups(dve, reduce)
            dve.wait_ge(up_reduced, GROUPS + 2)
            dve.wait_ge(z_ready, PAIRS + 1)
            dve.tensor_scalar(xm, flat_of(var), 1.0 / (NMEM - 1), 1.0, ALU.mult, ALU.add).then_inc(tail, 1)
            dve.wait_ge(tail, 1)
            dve.reciprocal(xm, xm).then_inc(tail, 1)
            dve.wait_ge(tail_exp, 1)
            dve.wait_ge(up_read, GROUPS + 2)
            dve.tensor_tensor(xm, xm, flat_of(mean), ALU.mult).then_inc(tail, 1)
            dve.wait_ge(tail, 3)
            dve.tensor_tensor(flat_of(var), xm, flat_of(xin), ALU.add).then_inc(tail, 1)

        @block.tensor
        def _(pe):
            pe.sem_inc(weighed, 2)
            pe.sem_inc(scored, KT)

            def norm(duo, s):
                pe.wait_ge(added, duo * 2 + 2)
                if not (isinstance(duo, int) and duo == 0):
                    pe.wait_ge(root, (duo - 1) * RSQ + 1)
                for g in range(4):
                    mm = pe.matmul(n_bank[32 * g:32 * g + 32, 0:2 * P], ones[:, 0:32], sumsq[s][:, :, :, 32 * g:32 * g + 32],
                                   start=True, stop=True)
                mm.then_inc(normed, 1)

            def scores(q, n, s, t):
                if t == 0:
                    pe.wait_ge(rest, q + 1)
                pe.wait_ge(exped, q * KT + (t + 1))
                for k, (part, c, te) in enumerate([(hi, 0, te_hi), (hi, 0, te_lo), (hi, 1, te_hi), (hi, 1, te_lo),
                                                   (lo, 0, te_hi), (lo, 1, te_hi)]):
                    mm = pe.matmul(s_bank[t][0:KP, 0:PIX], part[s][:, c, t * KP:(t + 1) * KP], te_part(te, n, c),
                                   start=(k == 0), stop=(k == 5))
                mm.then_inc(scored, 1)

            def weigh(q, u):
                pe.wait_ge(z_ready, q + 2)
                pe.wait_ge(exped, q * KT + 2 * KT)
                for t in range(KT):
                    mm = pe.matmul(pv_bank[u % 2][32 * t:32 * t + 32, 0:PIX], z[u % 2][:, t * ZC:(t + 1) * ZC], prob[u % 2][:, t, :],
                                   start=False, stop=False, skip_group_check=True)
                mm.then_inc(weighed, 1)

            def clear(n):
                pe.wait_ge(kept, n * 2 + 2)
                for g in range(2):
                    for t in range(KT):
                        pe.matmul(pv_bank[g][32 * t:32 * t + 32, 0:PIX], zeros[0:KP, 0:32], zeros[0:KP, 0:PIX],
                                  start=True, stop=False, skip_group_check=True)

            def gather(n):
                pe.wait_ge(kept, n * 2 + 2)
                pe.wait_ge(te_scaled, n * CC + CC)
                pe.wait_ge(lab_kept, n + 1)
                for w in range(6):
                    for g in range(2):
                        at = (2 * w + g) * ZC
                        mm = pe.matmul(m_bank[0:WP, at:at + ZC], sums[g][:, WINDOWS[w] * WF:WINDOWS[w] * WF + WP], sel[:, :],
                                       start=True, stop=True)
                mm.then_inc(gathered, 1)

            def turn_labels(n):
                pe.wait_ge(lab_sum, n * 2 + 2)
                for t in range(KT):
                    mm = pe.matmul(m_bank[0:KP, t * ZC:t * ZC + NMEM], lab_down[:, t * KP:(t + 1) * KP], ident[0:NMEM, 0:NMEM],
                                   start=True, stop=True)
                mm.then_inc(lab_turned, 1)

            def norm_test(n):
                pe.wait_ge(te_added, n + 1)
                if not (isinstance(n, int) and n == 0):
                    pe.wait_ge(lab_kept, n + 1)
                for g in range(4):
                    mm = pe.matmul(m_bank[32 * g:32 * g + 32, 0:P], ones[:, 0:32], te_ss[:, :, 32 * g:32 * g + 32],
                                   start=True, stop=True)
                mm.then_inc(te_normed, 1)

            def spread_test(n):
                pe.wait_ge(te_diaged, n * KT + KT)
                pe.matmul(m_bank[:, 0:PIX], ones[0:KP, :], te_diag[:, :, :].rearrange("p t k -> p (t k)"),
                          start=True, stop=True).then_inc(te_spread, 1)

            def body(n, i, first):
                for u in range(U):
                    q = n * NMEM + i * U + u
                    scores(q, n, u, 0)
                    scores(q, n, u, 1)
                    if u or not first:
                        weigh(n * NMEM + i * U + (u - 1), (u - 1) % U)
                    if u % 2:
                        norm(n * (NMEM // 2) + i * (U // 2) + (u + 3) // 2, (u + 3) % U // 2)
                    scores(q, n, u, 2)
                    scores(q, n, u, 3)
                    if first and u == 0:
                        clear(n)
                        gather(n)
                    if first and u == 2:
                        pe.wait_ge(divided, n * DIV + 2)
                        turn_labels(n + 1)
                    if first and u == 3:
                        norm_test(n + 1)
                    if first and u == 4:
                        spread_test(n + 1)

            pe.wait_ge(inited, 11)
            norm_test(0)
            norm(0, 0)
            pe.wait_ge(const_in, 48)
            spread_test(0)
            norm(1, 1)
            pe.wait_ge(te_scaled, CC)
            turn_labels(0)
            with pe.Fori(0, NSEQ) as n:
                pe.wait_ge(te_ready, n + 1)
                body(n, 0, first=True)
                with pe.Fori(1, BODIES) as i:
                    body(n, i, first=False)
                weigh(n * NMEM + (NMEM - 1), U - 1)
            gather(NSEQ)

            def upsample(g, h, jobs):
                pe.wait_ge(up_read, g + 1)
                for j, (w, k) in enumerate(jobs):
                    pe.matmul(psum[h][0:WL, j, 0:NCOL], up[:, k, :], down_hi[:, w, 32:COLS], start=True, stop=False)
                    mm = pe.matmul(psum[h][0:WL, j, 0:NCOL], up[:, k, :], down_lo[:, w, 32:COLS], start=False, stop=True)
                mm.then_inc(upped, 1)

            pe.wait_ge(exped, PAIRS * KT + KT)
            pe.wait_ge(up_ready, 1)
            pe.wait_ge(divided, (NSEQ + 1) * DIV)
            with pe.Fori(0, 5) as w:
                for v in range(4):
                    upsample(w * 4 + v, v % 2, [(w, 4 * v + k) for k in range(4)])
            upsample(20, 0, [(5, 12 + k) for k in range(4)])
            upsample(21, 1, [(0, 16), (0, 16), (5, 17), (5, 17)])


_INS = ["x", "L0_conv_train_labels", "L0_conv_test_feat", "L0_conv_train_feats", "L0_conv_softmax_temp"]


def kernel(**inputs):
    import numpy as np
    import concourse.bacc as bacc
    from concourse.bass_utils import run_bass_kernel_spmd

    nc = bacc.Bacc("TRN2", target_bir_lowering=False, num_devices=1)
    arrays = {name: np.ascontiguousarray(inputs[name]) for name in _INS}
    arrays |= {"c_ident": np.eye(P, dtype=np.float32), "c_sel": selector(), "c_up": upsampling()}
    args = [nc.dram_tensor(name, a.shape, mybir.dt.from_np(a.dtype), kind="ExternalInput").ap() for name, a in arrays.items()]
    out = nc.dram_tensor("out", (1, NSEQ, WL, HL), F32, kind="ExternalOutput").ap()
    build(nc, *args, out)
    r = run_bass_kernel_spmd(nc, [arrays], core_ids=[0])
    return r.results[0]["out"]
```

```python
from contextlib import ExitStack

import concourse.bass as bass
from concourse import mybir

ALU = mybir.AluOpType
ACT = mybir.ActivationFunctionType
AX = mybir.AxisListType
F32 = mybir.dt.float32
F32R = mybir.dt.float32r
I32 = mybir.dt.int32

P = 128
NMEM, NSEQ, C, WF, HF = 30, 16, 256, 22, 22
WL, HL = 88, 88
PIX = WF * HF
CC = C // P
KT = 4
KP = PIX // KT
ZC = 32
U = 6
BODIES = NMEM // U
PAIRS = NMEM * NSEQ
SLOT = NMEM + 1
NCOL = NSEQ * SLOT
COLS = 32 + NCOL
DIV = 7
SLOTS = 3
EARLY = 3
AHEAD = U - 1
ROWS = NMEM // 2
WIN = 5
WP = WIN * WF
WINDOWS = [4 * w for w in range(5)] + [HF - WIN]
UPS = 4
VAR = 16 + 2
ALPHA = 20.0
LIMIT = 64.0
STEPS = 3
RSQ = 3 + 3 * STEPS
MAGIC = 0x5F3759DF


def upsampling():
    import numpy as np

    def line(n_in, n_out):
        w = np.zeros((n_in, n_out), np.float32)
        for o in range(n_out):
            at = (o + 0.5) * n_in / n_out - 0.5
            lo = int(np.floor(at))
            for i, f in ((lo, 1 - (at - lo)), (lo + 1, at - lo)):
                w[min(max(i, 0), n_in - 1), o] += f
        return w

    rows = line(WF, WL)
    up = np.zeros((WIN, WF, VAR, WL), np.float32)
    for k in range(16):
        v, f = k // UPS, (k % UPS + 0.5) / UPS
        up[v, :, k] = (1 - f) * rows
        up[v + 1, :, k] = f * rows
    up[0, :, 16] = rows
    up[WIN - 1, :, 17] = rows
    return up.reshape(WP, VAR * WL)


def selector():
    import numpy as np

    s = np.zeros((KT, ZC // 2, 2, 2, ZC), np.float32)
    for r in range(ROWS):
        for d in range(2):
            s[:, r, d, d, r] = 1.0
    return s.reshape(P, 2 * ZC)


GROUPS = 22


def groups(eng, work):
    with eng.Fori(0, 5) as w:
        for v in range(4):
            work(w * 4 + v, v % 2, [(0, w * 16 + (2 + 4 * v), 4)])
    work(20, 0, [(0, 82, 4)])
    work(21, 1, [(0, 0, 2), (2, 86, 2)])


def build(nc, x, labels, test_feat, train_feats, temp, c_ident, c_sel, c_up, out):
    with ExitStack() as ctx:
        def sb(name, shape, dt=F32):
            return ctx.enter_context(nc.sbuf_tensor(name, shape, dt))

        def sem(name):
            return ctx.enter_context(nc.semaphore(name))

        raw_all = sb("raw_all", [P, U, CC, PIX])
        raw = [raw_all[:, s] for s in range(U)]
        hi_all = sb("hi_all", [P, U, CC, PIX], F32R)
        lo_all = sb("lo_all", [P, U, CC, PIX], F32R)
        hi, lo = ([part[:, s] for s in range(U)] for part in (hi_all, lo_all))
        sq_all = sb("sq_all", [P, 2, CC, PIX])
        sq = [sq_all[:, s] for s in range(2)]
        sumsq = [sb(f"sumsq{s}", [P, 2, KT, P]) for s in range(U // 2)]
        norms = sb("norms", [P, 2 * KT, 32])
        seed = sb("seed", [P, 2 * KT])
        root_a = sb("root_a", [P, 2 * KT])
        root_b = sb("root_b", [P, 2 * KT])
        rk = [sb(f"rk{s}", [P, 2 * KT]) for s in range(U // 2)]
        prob = [sb(f"prob{s}", [KP, KT, PIX]) for s in range(SLOTS)]
        z_all = sb("z_all", [KP, ROWS * 258])
        z_rows = z_all[:, :].rearrange("p (r x) -> p r x", r=ROWS)
        z_labels = z_rows[:, :, 0:256:ZC].rearrange("p r (b t) -> p r b t", b=2)
        z = [sb(f"z{s}", [KP, KT * ZC]) for s in range(SLOTS)]
        lab_raw = sb("lab_raw", [2 * 32, WF // 2, 2, HL])
        lab_down = sb("lab_down", [2 * 32, PIX // 2])
        lab = sb("lab", [KP, NMEM, KT])
        te_raw = sb("te_raw", [P, CC, PIX])
        te_sq = sb("te_sq", [P, CC, PIX])
        te_ss = sb("te_ss", [P, KT, P])
        te_norms = sb("te_norms", [P, KT, 32])
        te_rk = sb("te_rk", [P, KT])
        te_hi = sb("te_hi", [P, 2 * CC * PIX], F32R)
        te_lo = sb("te_lo", [P, 2 * CC * PIX], F32R)
        sums = [sb(f"sums{g}", [P, PIX]) for g in range(2)]
        rows = sb("rows", [P, PIX])
        lab_rows = rows[0:2 * 32, :].rearrange("p (y x q) -> p y x q", x=HF, q=2)
        te_diag = rows[0:KP, :].rearrange("p (t k) -> p t k", k=KP)
        rden = sb("rden", [WP, 6, NMEM])
        quot = sb("quot", [WP, 6, SLOT])
        dsum = sb("dsum", [WP, 6])
        dev = sb("dev", [WP, 6, COLS])
        ident = sb("ident", [P, P])
        ones = sb("ones", [P, P])
        sel = sb("sel", [P, 2 * ZC])
        tempc = sb("tempc", [P, 1])
        bias = sb("bias", [P, 1])
        hot = sb("hot", [1, 1], I32)
        tops = sb("tops", [KP, 2, PIX])
        top = tops[:, 1, :]

        flat = raw_all[:, :, :, :].rearrange("p u c k -> p (u c k)")
        up32 = flat[0:WP, 0:VAR * WL].rearrange("p (v y) -> p v y", v=VAR)
        at = VAR * WL
        xin, mean, var = (
            flat[0:WL, at + NSEQ * HL * b:at + NSEQ * HL * (b + 1)].rearrange("p (n x) -> p n x", x=HL)
            for b in range(3)
        )
        xm = z_all[0:WL, 0:NSEQ * HL]
        up_sq = [prob[b][0:WL, :, 0:PAIRS].rearrange("p j (n m) -> p j n m", m=NMEM) for b in range(2)]
        up = te_hi[0:WP, 0:VAR * WL].rearrange("p (v y) -> p v y", v=VAR)
        dev_hi, dev_lo = (part[:, :, :, :].rearrange("p u c k -> p (u c k)")[0:WP, 0:6 * COLS].rearrange("p (w c) -> p w c", w=6)
                          for part in (hi_all, lo_all))

        psum = [ctx.enter_context(nc.psum_tensor(f"banks{h}", [P, 4, 512], F32)) for h in range(2)]
        s_bank = [psum[0][:, t] for t in range(KT)]
        n_bank, pv_bank, m_bank = psum[1][:, 0], (psum[1][:, 1], psum[1][:, 2]), psum[1][:, 3]

        const_in, lab_in, te_in, x_in = sem("const_in"), sem("lab_in"), sem("te_in"), sem("x_in")
        tr_in = [sem(f"tr_in{s}") for s in range(U)]
        inited = sem("inited")
        lab_sum, lab_turned, lab_kept = sem("lab_sum"), sem("lab_turned"), sem("lab_kept")
        squared, rounded, rest, added = sem("squared"), sem("rounded"), sem("rest"), sem("added")
        normed, root = sem("normed"), sem("root")
        scored, exped, z_built, z_ready, weighed = (sem(k) for k in ("scored", "exped", "z_built", "z_ready", "weighed"))
        kept, gathered, sums_turned, divided = (sem(k) for k in ("kept", "gathered", "sums_turned", "divided"))
        te_squared, te_added, te_normed, te_diaged, te_spread = (
            sem(k) for k in ("te_squared", "te_added", "te_normed", "te_diaged", "te_spread"))
        te_root, te_scaled, te_rounded, te_ready = (sem(k) for k in ("te_root", "te_scaled", "te_rounded", "te_ready"))
        up_ready, upped, up_squared, up_read, up_reduced = (
            sem(k) for k in ("up_ready", "upped", "up_squared", "up_read", "up_reduced"))
        hot_ready, scaled, maxed, reduced, lowered = (sem(k) for k in ("hot_ready", "scaled", "maxed", "reduced", "lowered"))
        dev_rounded, dev_split = sem("dev_rounded"), sem("dev_split")
        tail, tail_exp, out_done = sem("tail"), sem("tail_exp"), sem("out_done")

        tr_v = train_feats.rearrange("m n (p c) h w -> m n p c (h w)", c=CC)
        te_v = test_feat.rearrange("o n (p c) h w -> (o n) p c (h w)", c=CC)
        lab_v = labels.rearrange("m n (h y r) x -> n h m y r x", h=2, r=UPS)

        def tiles_of(ap):
            return ap.rearrange("p (t k) -> p t k", t=KT)

        def flat_of(ap):
            return ap.rearrange("p n x -> p (n x)")

        def te_part(part, n, c):
            return part[:, bass.ds(n % 2 * (CC * PIX) + c * PIX, PIX)]

        def either(eng, sequences):
            eng.wait_ge(hot_ready, 1)
            is_hot = eng.value_load(hot[0:1, 0:1], min_val=0, max_val=1)
            with eng.If(is_hot == 0):
                sequences(guarded=False)
            with eng.Else():
                sequences(guarded=True)

        block = ctx.enter_context(nc.Block())

        @block.sync
        def _(sp):
            def labels_of(n):
                for h in range(2):
                    sp.dma_start(lab_raw[32 * h:32 * h + NMEM, :, :, :], lab_v[n, h, :, :, 1:3, :]).then_inc(lab_in, 16)

            def next_test(n):
                sp.dma_start(te_raw[:, :, :], te_v[n]).then_inc(te_in, 16)
                labels_of(n)

            sp.dma_start(te_raw[:, :, :], te_v[0]).then_inc(te_in, 16)
            for u in range(2):
                sp.dma_start(raw[u], tr_v[u, 0]).then_inc(tr_in[u], 16)
            sp.dma_start(ident[:, :], c_ident).then_inc(const_in, 16)
            sp.dma_start(sel[:, :], c_sel).then_inc(const_in, 16)
            sp.dma_start(tempc[:, :], temp.rearrange("(o t) -> o t", o=1).broadcast_to((P, 1))).then_inc(const_in, 16)
            sp.wait_ge(inited, 4)
            labels_of(0)
            for u in range(2, U):
                sp.dma_start(raw[u], tr_v[u, 0]).then_inc(tr_in[u], 16)

            def refill(q, m, n, u):
                sp.wait_ge(squared, q - U + 1)
                sp.wait_ge(rounded, q - U + 1)
                sp.wait_ge(rest, q - U + 1)
                sp.dma_start(raw[u], tr_v[m, n]).then_inc(tr_in[u], 16)

            def bodies(n, i0):
                with sp.Fori(i0, BODIES) as i:
                    for u in range(U):
                        refill(n * NMEM + i * U + u, i * U + u, n, u)

            def test_free(n):
                sp.wait_ge(te_scaled, n * CC)
                sp.wait_ge(lab_sum, n * 2)

            test_free(1)
            next_test(1)
            bodies(0, 1)
            with sp.Fori(1, NSEQ - 1) as n:
                test_free(n + 1)
                next_test(n + 1)
                bodies(n, 0)
            test_free(NSEQ)
            next_test(0)
            bodies(NSEQ - 1, 0)
            for u in range(AHEAD):
                refill(PAIRS + u, u, 0, u)
            sp.wait_ge(squared, PAIRS + AHEAD)
            sp.wait_ge(rounded, PAIRS + AHEAD)
            sp.wait_ge(rest, PAIRS + AHEAD)
            sp.dma_start(up32, c_up.rearrange("p (v y) -> p v y", v=VAR)).then_inc(x_in, 16)
            sp.dma_start(xin, x.rearrange("o n y x -> y (o n) x")).then_inc(x_in, 16)
            sp.wait_ge(tail, 4)
            sp.dma_start(out.rearrange("o n y x -> y (o n) x"), var).then_inc(out_done, 16)
            sp.wait_ge(out_done, 16)

        @block.scalar
        def _(act):
            act.sem_inc(exped, KT)

            def square(q, s, loads, late=True):
                act.wait_ge(tr_in[s], loads * 16)
                if late or q >= 2:
                    act.wait_ge(added, q - 1)
                act.activation(sq[s % 2], raw[s], ACT.Square).then_inc(squared, 1)

            def round_up(q, s, late=True):
                if late:
                    act.wait_ge(scored, (q - U + 2) * KT)
                act.copy(hi[s][:, :, :], raw[s]).then_inc(rounded, 1)

            def exps(q, duo, u, tiles):
                if 0 in tiles:
                    act.wait_ge(root, (duo + 1) * RSQ)
                    act.wait_ge(weighed, q + 1)
                for t in tiles:
                    act.wait_ge(scored, q * KT + (KT + t + 1))
                    act.activation(prob[u % SLOTS][:, t, :], s_bank[t][0:KP, 0:PIX], ACT.Exp,
                                   scale=rk[u // 2][0:KP, (u % 2) * KT + t:(u % 2) * KT + t + 1]).then_inc(exped, 1)

            def guarded_exps(q, duo, u):
                act.wait_ge(root, (duo + 1) * RSQ)
                act.wait_ge(weighed, q + 1)
                for t in range(KT):
                    act.wait_ge(scored, q * KT + (KT + t + 1))
                    act.activation(prob[u % SLOTS][:, t, :], s_bank[t][0:KP, 0:PIX], ACT.Copy,
                                   scale=rk[u // 2][0:KP, (u % 2) * KT + t:(u % 2) * KT + t + 1]).then_inc(scaled, 1)
                for t in range(KT):
                    act.wait_ge(lowered, q * KT + t + 1)
                    act.activation(prob[u % SLOTS][:, t, :], prob[u % SLOTS][:, t, :], ACT.Exp).then_inc(exped, 1)

            def square_test(n):
                act.wait_ge(te_in, n * 16 + 16)
                act.activation(te_sq[:, :, :], te_raw[:, :, :], ACT.Square).then_inc(te_squared, 1)

            def body(n, i, guarded, beside=None):
                for u in range(U):
                    q = n * NMEM + i * U + u
                    duo = n * (NMEM // 2) + i * (U // 2) + u // 2
                    if not guarded:
                        exps(q, duo, u, (0, 1))
                    square(q + AHEAD, (u + AHEAD) % U, n * BODIES + i + ((u + AHEAD) // U + 1))
                    round_up(q + AHEAD, (u + AHEAD) % U)
                    if guarded:
                        guarded_exps(q, duo, u)
                    else:
                        exps(q, duo, u, (2, 3))
                    if beside == "test" and u == 0:
                        act.wait_ge(te_ready, n + 1)
                        square_test(n + 1)

            square_test(0)
            for q in range(AHEAD):
                square(q, q, 1, late=False)
                round_up(q, q, late=False)

            def sequences(guarded):
                with act.Fori(0, NSEQ) as n:
                    with act.Fori(0, EARLY) as i:
                        body(n, i, guarded)
                    body(n, EARLY, guarded, beside="test")
                    with act.Fori(EARLY + 1, BODIES) as i:
                        body(n, i, guarded)

            either(act, sequences)

            def read_up(g, h, pieces):
                act.wait_ge(upped, g + 1)
                act.wait_ge(up_reduced, g + 1)
                cols = psum[h][0:WL, :, 0:NCOL].rearrange("p j (n m) -> p j n m", m=SLOT)
                act.activation(up_sq[h], cols[:, :, :, 0:NMEM], ACT.Square).then_inc(up_squared, 1)
                for j0, x0, k in pieces:
                    last = act.copy(mean[:, :, bass.ds(x0, k)].rearrange("p n x -> p x n"), cols[:, j0:j0 + k, :, NMEM])
                last.then_inc(up_read, 1)

            act.wait_ge(x_in, 32)
            act.wait_ge(scored, PAIRS * KT + KT)
            act.wait_ge(te_ready, NSEQ + 1)
            act.copy(up, up32).then_inc(up_ready, 1)
            act.wait_ge(rest, PAIRS + AHEAD)
            act.wait_ge(divided, (NSEQ + 1) * DIV)
            for w in range(6):
                act.copy(dev_hi[:, w, 32:COLS], dev[:, w, 32:COLS]).then_inc(dev_rounded, 1)
            act.sem_inc(up_read, 2)
            act.wait_ge(weighed, PAIRS + 3)
            groups(act, read_up)
            act.wait_ge(tail, 2)
            act.activation(xm, xm, ACT.Exp, scale=ALPHA, bias=bias[0:WL, 0:1]).then_inc(tail_exp, 1)

        @block.gpsimd
        def _(pool):
            pool.memset(te_ss[:, :, :], 1.0).then_inc(inited, 1)
            pool.memset(sumsq[0][:, :, :, :], 1.0).then_inc(inited, 1)
            pool.memset(ones[:, :], 1.0).then_inc(inited, 1)
            pool.memset(lab_raw[:, :, :, :], 0.0).then_inc(inited, 1)
            for s in range(1, U // 2):
                pool.memset(sumsq[s][:, :, :, :], 1.0).then_inc(inited, 1)
            pool.memset(z_all[:, :], 0.0).then_inc(inited, 1)
            pool.memset(sums[0][:, :], 1.0).then_inc(inited, 1)
            pool.memset(z[-1][:, :], 0.0).then_inc(inited, 1)
            pool.memset(prob[-1][:, :, :], 0.0).then_inc(inited, 1)
            pool.memset(bias[:, :], -ALPHA).then_inc(inited, 1)
            pool.wait_ge(inited, 7)
            pool.memset(z_rows[:, :, 1:257:ZC], 1.0).then_inc(inited, 1)
            pool.sem_inc(z_ready, 1)

            def sequences(guarded):
                with pool.Fori(0, NSEQ) as n:
                    with pool.Fori(0, BODIES) as i:
                        pool.wait_ge(z_built, n + 1)
                        for u in range(U):
                            q = n * NMEM + i * U + u
                            if guarded:
                                pool.wait_ge(maxed, q * 3 + 3)
                            pool.wait_ge(weighed, q + 1)
                            pool.tensor_copy(z[u % SLOTS][:, :], z_all[:, bass.ds((i * U + u) * (KT * ZC), KT * ZC)]).then_inc(z_ready, 1)
                            if guarded:
                                pool.partition_all_reduce(top, tops[:, 0, :], KP, bass.bass_isa.ReduceOp.max).then_inc(reduced, 1)

            either(pool, sequences)

        @block.vector
        def _(dve):
            def newton(r, a, b, square, out, s, base):
                bits = r.bitcast(I32)
                dve.tensor_scalar(bits, square.bitcast(I32), 1, None, ALU.arith_shift_right).then_inc(s, 1)
                dve.wait_ge(s, base + 1)
                dve.tensor_scalar(bits, bits, -1.0, float(MAGIC), ALU.mult, ALU.add).then_inc(s, 1)
                for k in range(STEPS):
                    at = base + (2 + 3 * k)
                    dve.wait_ge(s, at)
                    dve.tensor_tensor(a, r, r, ALU.mult).then_inc(s, 1)
                    dve.wait_ge(s, at + 1)
                    dve.scalar_tensor_tensor(out=b, in0=a, scalar=-0.5, in1=square, op0=ALU.mult, op1=ALU.mult).then_inc(s, 1)
                    dve.wait_ge(s, at + 2)
                    dve.scalar_tensor_tensor(out=out if k == STEPS - 1 else r, in0=b, scalar=1.5, in1=r,
                                             op0=ALU.add, op1=ALU.mult).then_inc(s, 1)

            def add(q, s):
                dve.wait_ge(squared, q + 1)
                dve.tensor_tensor(sumsq[s // 2][:, s % 2, :, 0:KP], tiles_of(sq[s % 2][:, 0, :]), tiles_of(sq[s % 2][:, 1, :]),
                                  ALU.add).then_inc(added, 1)

            def take_rest(q, s):
                dve.wait_ge(rounded, q + 1)
                dve.tensor_tensor(lo[s], raw[s], hi[s].bitcast(F32), ALU.subtract).then_inc(rest, 1)

            def roots(duo, s, late=True):
                dve.wait_ge(normed, duo + 1)
                dve.transpose(norms[:, :, :].rearrange("p a b -> p (a b)"), n_bank[:, 0:2 * P]).then_inc(root, 1)
                dve.wait_ge(root, duo * RSQ + 1)
                if late:
                    dve.wait_ge(weighed, duo * 2 - 1)
                newton(seed[:, :], root_a[:, :], root_b[:, :], norms[:, :, 0], rk[s][:, :], root, duo * RSQ + 1)

            def add_labels(n):
                dve.wait_ge(lab_in, n * 32 + 32)
                mid = lab_raw[:, :, :, :].rearrange("p y r (x q) -> p y r x q", q=UPS)
                dve.tensor_tensor(lab_rows, mid[:, :, 0, :, 1:3], mid[:, :, 1, :, 1:3], ALU.add).then_inc(lab_sum, 1)
                dve.wait_ge(lab_sum, n * 2 + 1)
                dve.tensor_tensor(lab_down[:, :].rearrange("p (y x) -> p y x", x=HF), lab_rows[:, :, :, 0], lab_rows[:, :, :, 1],
                                  ALU.add).then_inc(lab_sum, 1)

            def keep_labels(n):
                dve.wait_ge(lab_turned, n + 1)
                dve.tensor_scalar(lab[:, :, :].rearrange("p m (h a) -> p a h m", h=2),
                                  m_bank[0:KP, 0:2 * 64].rearrange("p (a h m) -> p a h m", a=2, h=2)[:, :, :, 0:NMEM], 0.25, None,
                                  ALU.mult).then_inc(lab_kept, 1)

            def add_test(n):
                dve.wait_ge(te_squared, n + 1)
                dve.tensor_tensor(te_ss[:, :, 0:KP], tiles_of(te_sq[:, 0, :]), tiles_of(te_sq[:, 1, :]), ALU.add).then_inc(te_added, 1)

            def root_test(n):
                dve.wait_ge(te_normed, n + 1)
                dve.transpose(te_norms[:, :, :].rearrange("p a b -> p (a b)"), m_bank[:, 0:P]).then_inc(te_root, 1)
                dve.wait_ge(te_root, n * RSQ + 1)
                newton(seed[:, 0:KT], root_a[:, 0:KT], root_b[:, 0:KT], te_norms[:, :, 0], te_rk[:, :], te_root, n * RSQ + 1)

            def test_diagonals(n):
                dve.wait_ge(te_root, n * RSQ + RSQ)
                for t in range(KT):
                    dve.tensor_scalar(te_diag[:, t, :], ident[0:KP, 0:KP], te_rk[0:KP, t:t + 1], None, ALU.mult).then_inc(te_diaged, 1)

            def scale_test(n, c):
                dve.wait_ge(te_spread, n + 1)
                dve.scalar_tensor_tensor(out=te_sq[:, c, :].rearrange("p (x y) -> p x y", x=HF),
                                         in0=te_raw[:, c, :].rearrange("p (y x) -> p x y", y=WF),
                                         scalar=tempc[:, 0:1],
                                         in1=m_bank[:, 0:PIX].rearrange("p (y x) -> p x y", y=WF),
                                         op0=ALU.mult, op1=ALU.mult).then_inc(te_scaled, 1)

            def round_test(n):
                dve.wait_ge(te_scaled, n * CC + CC)
                at = n % 2 * (CC * PIX)
                whole = te_sq[:, :, :].rearrange("p c k -> p (c k)")
                dve.tensor_copy(te_hi[:, bass.ds(at, CC * PIX)], whole).then_inc(te_rounded, 1)
                dve.wait_ge(te_rounded, n + 1)
                dve.tensor_tensor(te_lo[:, bass.ds(at, CC * PIX)], whole, te_hi[:, :].bitcast(F32)[:, bass.ds(at, CC * PIX)],
                                  ALU.subtract).then_inc(te_ready, 1)

            def take_sums(n):
                dve.wait_ge(gathered, n + 2)
                dve.tensor_copy(rows[:, :], m_bank[:, 0:PIX]).then_inc(divided, 1)

            turned = m_bank[0:WP, 0:6 * 4 * ROWS].rearrange("p (w d m) -> p w d m", w=6, d=2)

            def invert(n):
                dve.wait_ge(sums_turned, n + 1)
                dve.reciprocal(rden[:, :, :], turned[:, :, 1, :]).then_inc(divided, 1)

            def divide(n):
                dve.wait_ge(divided, n * DIV + 2)
                dve.tensor_tensor(quot[:, :, 0:NMEM], turned[:, :, 0, :], rden[:, :, :], ALU.mult).then_inc(divided, 1)

            def centre(n):
                each = quot[:, :, 0:NMEM]
                dve.wait_ge(divided, n * DIV + 3)
                dve.tensor_reduce(dsum[:, :], each, AX.X, ALU.add).then_inc(divided, 1)
                dve.wait_ge(divided, n * DIV + 4)
                dve.tensor_scalar(quot[:, :, NMEM], dsum[:, :], 1.0 / NMEM, None, ALU.mult).then_inc(divided, 1)
                dve.wait_ge(divided, n * DIV + 5)
                dve.tensor_tensor(each, each, quot[:, :, NMEM:SLOT].broadcast_to((WP, 6, NMEM)), ALU.subtract).then_inc(divided, 1)
                dve.wait_ge(divided, n * DIV + 6)
                dve.tensor_copy(dev[:, :, bass.ds(n * SLOT + 1, SLOT)], quot[:, :, :]).then_inc(divided, 1)

            def lower(q, u):
                dve.wait_ge(scaled, q * KT + KT)
                dve.tensor_tensor(tops[:, 0, :], prob[u % SLOTS][:, 0, :], prob[u % SLOTS][:, 1, :], ALU.max).then_inc(maxed, 1)
                dve.tensor_tensor(tops[:, 1, :], prob[u % SLOTS][:, 2, :], prob[u % SLOTS][:, 3, :], ALU.max).then_inc(maxed, 1)
                dve.wait_ge(maxed, q * 3 + 2)
                dve.tensor_tensor(tops[:, 0, :], tops[:, 0, :], tops[:, 1, :], ALU.max).then_inc(maxed, 1)
                dve.wait_ge(reduced, q + 1)
                for t in range(KT):
                    dve.tensor_tensor(prob[u % SLOTS][:, t, :], prob[u % SLOTS][:, t, :], top, ALU.subtract).then_inc(lowered, 1)

            def label_tiles(n):
                dve.wait_ge(lab_kept, n + 1)
                dve.wait_ge(z_ready, n * NMEM + 1)
                dve.tensor_copy(z_labels, lab[:, :, :].rearrange("p (r b) t -> p r b t", b=2)).then_inc(z_built, 1)

            def keep_sums(n, g):
                dve.wait_ge(weighed, n * NMEM + (2 + g))
                dve.wait_ge(gathered, n + 1)
                dve.tensor_copy(sums[g][:, :], pv_bank[g][:, 0:PIX]).then_inc(kept, 1)

            def body(n, i, guarded, beside=None):
                for u in range(U):
                    if beside == "sums" and u == 0:
                        label_tiles(n)
                        keep_sums(n, 0)
                    if beside == "sums" and u == 2:
                        keep_sums(n, 1)
                    if beside == "sums" and u == 4:
                        take_sums(n)
                    if beside == "test" and u == 0:
                        add_labels(n + 1)
                    if beside == "test" and u == 2:
                        keep_labels(n + 1)
                        add_test(n + 1)
                    if beside == "test" and u == 4:
                        root_test(n + 1)
                    if beside == "test" and u == 5:
                        test_diagonals(n + 1)
                    v = u + AHEAD
                    add(n * NMEM + i * U + v, v % U)
                    take_rest(n * NMEM + i * U + v, v % U)
                    if u % 2 == 0:
                        roots(n * (NMEM // 2) + i * (U // 2) + (u + 2) // 2, (u + 2) % U // 2)
                    if guarded:
                        lower(n * NMEM + i * U + u, u)

            dve.wait_ge(inited, 1)
            add_test(0)
            dve.wait_ge(inited, 2)
            add(0, 0)
            take_rest(0, 0)
            dve.wait_ge(const_in, 48)
            dve.tensor_scalar(hot[:, :], tempc[0:1, :], tempc[0:1, 0:1], LIMIT * LIMIT, ALU.mult, ALU.is_gt).then_inc(hot_ready, 1)
            root_test(0)
            test_diagonals(0)
            add(1, 1)
            take_rest(1, 1)
            roots(0, 0, late=False)
            scale_test(0, 0)
            scale_test(0, 1)
            round_test(0)
            dve.wait_ge(inited, 6)
            add(2, 2)
            take_rest(2, 2)
            add_labels(0)
            add(3, 3)
            take_rest(3, 3)
            keep_labels(0)
            add(4, 4)
            take_rest(4, 4)
            dve.wait_ge(inited, 12)

            def sequences(guarded):
                with dve.Fori(0, NSEQ) as n:
                    body(n, 0, guarded, beside="sums")
                    invert(n)
                    divide(n)
                    centre(n)
                    with dve.Fori(1, EARLY) as i:
                        body(n, i, guarded)
                    body(n, EARLY, guarded, beside="test")
                    for c in range(CC):
                        scale_test(n + 1, c)
                    round_test(n + 1)
                    with dve.Fori(EARLY + 1, BODIES) as i:
                        body(n, i, guarded)

            either(dve, sequences)
            for g in range(2):
                keep_sums(NSEQ, g)
            take_sums(NSEQ)
            invert(NSEQ)
            divide(NSEQ)
            centre(NSEQ)
            dve.wait_ge(scored, PAIRS * KT + KT)
            for w in range(6):
                dve.wait_ge(dev_rounded, w + 1)
                dve.tensor_tensor(dev_lo[:, w, 32:COLS], dev[:, w, 32:COLS], dev_hi[:, w, 32:COLS].bitcast(F32),
                                  ALU.subtract).then_inc(dev_split, 1)

            def reduce(g, h, pieces):
                dve.wait_ge(up_squared, g + 1)
                for j0, x0, k in pieces:
                    last = dve.tensor_reduce(var[:, :, bass.ds(x0, k)].rearrange("p n x -> p x n"), up_sq[h][:, j0:j0 + k], AX.X,
                                             ALU.add)
                last.then_inc(up_reduced, 1)

            dve.sem_inc(up_reduced, 2)
            groups(dve, reduce)
            dve.wait_ge(up_reduced, GROUPS + 2)
            dve.wait_ge(z_ready, PAIRS + 1)
            dve.tensor_scalar(xm, flat_of(var), 1.0 / (NMEM - 1), 1.0, ALU.mult, ALU.add).then_inc(tail, 1)
            dve.wait_ge(tail, 1)
            dve.reciprocal(xm, xm).then_inc(tail, 1)
            dve.wait_ge(tail_exp, 1)
            dve.wait_ge(up_read, GROUPS + 2)
            dve.tensor_tensor(xm, xm, flat_of(mean), ALU.mult).then_inc(tail, 1)
            dve.wait_ge(tail, 3)
            dve.tensor_tensor(flat_of(var), xm, flat_of(xin), ALU.add).then_inc(tail, 1)

        @block.tensor
        def _(pe):
            pe.sem_inc(gathered, 1)
            pe.sem_inc(scored, KT)

            def norm(duo, s):
                pe.wait_ge(added, duo * 2 + 2)
                if not (isinstance(duo, int) and duo == 0):
                    pe.wait_ge(root, (duo - 1) * RSQ + 1)
                for g in range(4):
                    mm = pe.matmul(n_bank[32 * g:32 * g + 32, 0:2 * P], ones[:, 0:32], sumsq[s][:, :, :, 32 * g:32 * g + 32],
                                   start=True, stop=True)
                mm.then_inc(normed, 1)

            def scores(q, n, s, t):
                if t == 0:
                    pe.wait_ge(rest, q + 1)
                pe.wait_ge(exped, q * KT + (t + 1))
                for k, (part, c, te) in enumerate([(hi, 0, te_hi), (hi, 0, te_lo), (hi, 1, te_hi), (hi, 1, te_lo),
                                                   (lo, 0, te_hi), (lo, 1, te_hi)]):
                    mm = pe.matmul(s_bank[t][0:KP, 0:PIX], part[s][:, c, t * KP:(t + 1) * KP], te_part(te, n, c),
                                   start=(k == 0), stop=(k == 5))
                mm.then_inc(scored, 1)

            def weigh(q, u, start=False):
                pe.wait_ge(z_ready, q + 2)
                pe.wait_ge(exped, q * KT + 2 * KT)
                for t in range(KT):
                    mm = pe.matmul(pv_bank[u % 2][32 * t:32 * t + 32, 0:PIX], z[u % SLOTS][:, t * ZC:(t + 1) * ZC], prob[u % SLOTS][:, t, :],
                                   start=start, stop=False, skip_group_check=True)
                mm.then_inc(weighed, 1)

            def gather(n):
                pe.wait_ge(kept, n * 2 + 2)
                pe.wait_ge(te_scaled, n * CC + CC)
                pe.wait_ge(lab_kept, n + 1)
                for d in range(2):
                    for g in range(2):
                        at = 2 * ZC * d + ZC * g
                        mm = pe.matmul(m_bank[at:at + ZC, 0:PIX], sel[:, ZC * d:ZC * d + ZC], sums[g][:, :], start=True, stop=True)
                mm.then_inc(gathered, 1)

            def turn_sums(n):
                pe.wait_ge(divided, n * DIV + 1)
                used = ident[:, :].rearrange("p (b r) -> p b r", b=4)[:, :, 0:ROWS]
                for w in range(6):
                    mm = pe.matmul(m_bank[0:WP, 4 * ROWS * w:4 * ROWS * w + 4 * ROWS], rows[:, WINDOWS[w] * WF:WINDOWS[w] * WF + WP],
                                   used, start=True, stop=True)
                mm.then_inc(sums_turned, 1)

            def turn_labels(n):
                pe.wait_ge(lab_sum, n * 2 + 2)
                for a in range(2):
                    mm = pe.matmul(m_bank[0:KP, a * 64:a * 64 + 62], lab_down[0:62, a * KP:(a + 1) * KP], ident[0:62, 0:62],
                                   start=True, stop=True)
                mm.then_inc(lab_turned, 1)

            def norm_test(n):
                pe.wait_ge(te_added, n + 1)
                if not (isinstance(n, int) and n == 0):
                    pe.wait_ge(lab_kept, n + 1)
                for g in range(4):
                    mm = pe.matmul(m_bank[32 * g:32 * g + 32, 0:P], ones[:, 0:32], te_ss[:, :, 32 * g:32 * g + 32],
                                   start=True, stop=True)
                mm.then_inc(te_normed, 1)

            def spread_test(n):
                pe.wait_ge(te_diaged, n * KT + KT)
                pe.matmul(m_bank[:, 0:PIX], ones[0:KP, :], rows[0:KP, :],
                          start=True, stop=True).then_inc(te_spread, 1)

            def body(n, i, beside=None):
                for u in range(U):
                    q = n * NMEM + i * U + u
                    for t in range(KT):
                        scores(q, n, u, t)
                    if u % 2:
                        if beside == "sums" and u in (1, 3):
                            pe.wait_ge(kept, n * 2 + (u + 1) // 2)
                        weigh(q - 2, u - 2, start=beside == "sums" and u == 3)
                        weigh(q - 1, u - 1, start=beside == "sums" and u == 1)
                        norm(n * (NMEM // 2) + i * (U // 2) + (u + 3) // 2, (u + 3) % U // 2)
                    if beside == "sums" and u == 3:
                        gather(n)
                    if beside == "sums" and u == 5:
                        turn_sums(n)
                    if beside == "test" and u == 1:
                        pe.wait_ge(divided, n * DIV + 3)
                        turn_labels(n + 1)
                    if beside == "test" and u == 3:
                        norm_test(n + 1)
                    if beside == "test" and u == 5:
                        spread_test(n + 1)

            pe.wait_ge(inited, 3)
            norm_test(0)
            norm(0, 0)
            pe.wait_ge(const_in, 48)
            spread_test(0)
            norm(1, 1)
            pe.wait_ge(te_scaled, CC)
            turn_labels(0)
            pe.wait_ge(inited, 12)
            for g in range(2):
                pe.matmul(pv_bank[g][:, 0:PIX], ones[:, :], sums[0][:, :], start=True, stop=False, skip_group_check=True).then_inc(weighed, 1)
            with pe.Fori(0, NSEQ) as n:
                pe.wait_ge(te_ready, n + 1)
                body(n, 0, beside="sums")
                with pe.Fori(1, EARLY) as i:
                    body(n, i)
                body(n, EARLY, beside="test")
                with pe.Fori(EARLY + 1, BODIES) as i:
                    body(n, i)
            weigh(PAIRS - 1, U - 1)
            gather(NSEQ)
            turn_sums(NSEQ)

            def upsample(g, h, jobs):
                pe.wait_ge(up_read, g + 1)
                for j, (w, k) in enumerate(jobs):
                    pe.matmul(psum[h][0:WL, j, 0:NCOL], up[:, k, :], dev_hi[:, w, 32:COLS], start=True, stop=False)
                    mm = pe.matmul(psum[h][0:WL, j, 0:NCOL], up[:, k, :], dev_lo[:, w, 32:COLS], start=False, stop=True)
                mm.then_inc(upped, 1)

            pe.wait_ge(exped, PAIRS * KT + KT)
            pe.wait_ge(up_ready, 1)
            with pe.Fori(0, 5) as w:
                pe.wait_ge(dev_split, w + 1)
                for v in range(4):
                    upsample(w * 4 + v, v % 2, [(w, 4 * v + k) for k in range(4)])
            pe.wait_ge(dev_split, 6)
            upsample(20, 0, [(5, 12 + k) for k in range(4)])
            upsample(21, 1, [(0, 16), (0, 16), (5, 17), (5, 17)])


_INS = ["x", "L0_conv_train_labels", "L0_conv_test_feat", "L0_conv_train_feats", "L0_conv_softmax_temp"]


def kernel(**inputs):
    import numpy as np
    import concourse.bacc as bacc
    from concourse.bass_utils import run_bass_kernel_spmd

    nc = bacc.Bacc("TRN2", target_bir_lowering=False, num_devices=1)
    arrays = {name: np.ascontiguousarray(inputs[name]) for name in _INS}
    arrays |= {"c_ident": np.eye(P, dtype=np.float32), "c_sel": selector(), "c_up": upsampling()}
    args = [nc.dram_tensor(name, a.shape, mybir.dt.from_np(a.dtype), kind="ExternalInput").ap() for name, a in arrays.items()]
    out = nc.dram_tensor("out", (1, NSEQ, WL, HL), F32, kind="ExternalOutput").ap()
    build(nc, *args, out)
    r = run_bass_kernel_spmd(nc, [arrays], core_ids=[0])
    return r.results[0]["out"]
```
